# Optimizing a Trainium2 kernel written in Bass

```python
import numpy as np
import jax
import jax.numpy as jnp

def _softmax(x, axis=-1):
    return jax.nn.softmax(x, axis=axis)

def _gelu(x):
    return jax.nn.gelu(x, approximate=True)

def _silu(x):
    return jax.nn.silu(x)

def _sigmoid(x):
    return jax.nn.sigmoid(x)

def _layernorm(x, axis=-1, eps=1e-05):
    m = jnp.mean(x, axis=axis, keepdims=True)
    v = jnp.var(x, axis=axis, keepdims=True)
    return (x - m) / jnp.sqrt(v + eps)

def _scatter_add(tgt, idx, src, axis=0):
    return tgt.at[idx].add(src)

def _segment_sum(src, seg, n):
    return jax.ops.segment_sum(src, seg, n)
kernel_name = 'mk_gnn_resnorm_d2_gnn_r8_6cd23a'

def setup_inputs(seed: int=0):
    np.random.seed(seed)
    _w = jnp.asarray

    def _rec_inputs():
        import jax
        import jax.numpy as jnp
        _gk = jax.random.key(seed)
        x = -0.0005121 + 1.001 * jax.random.normal(jax.random.fold_in(_gk, 1), (6250, 160), jnp.float32)
        _s = jax.random.randint(jax.random.fold_in(_gk, 2), (100000,), 0, 6250, jnp.int32)
        _d = jax.random.randint(jax.random.fold_in(_gk, 3), (100000,), 0, 6250, jnp.int32)
        _loop = jnp.arange(6250, dtype=jnp.int32)
        src = jnp.concatenate([_s, _d, _loop])
        dst = jnp.concatenate([_d, _s, _loop])
        _o = jnp.argsort(dst, stable=True)
        src = src[_o]
        dst = dst[_o]
        edge_attr_10 = jax.random.uniform(jax.random.fold_in(_gk, 12), (206250, 10), jnp.float32, 0.0, 1)
        edge_attr_16 = -0.000191324 + 0.999809 * jax.random.normal(jax.random.fold_in(_gk, 13), (206250, 16), jnp.float32)
        edge_attr_4 = 0.000126197 + 0.999763 * jax.random.normal(jax.random.fold_in(_gk, 14), (206250, 4), jnp.float32)
        node_vec1 = jax.random.uniform(jax.random.fold_in(_gk, 15), (6250, 1), jnp.float32, 0.0, 1)
        return (x, src, dst, edge_attr_10, edge_attr_16, edge_attr_4, node_vec1)
    x, src, dst, edge_attr_10, edge_attr_16, edge_attr_4, node_vec1 = _rec_inputs()

    def _L0_gnn_setup():
        import jax, jax.numpy as jnp
        import numpy as np
        N = 2500
        E = 40000
        MUL0 = 64
        MUL1 = 32
        FC_IN = 16
        FC_H = 64
        WNUM = 192
        key = jax.random.key(seed)
        ks = jax.random.split(key, 16)
        return {'x': jax.random.normal(ks[0], (N, MUL0 + 3 * MUL1), jnp.float32), 'node_attr': jnp.ones((N, 1), jnp.float32), 'edge_scalars': jax.random.normal(ks[1], (E, FC_IN), jnp.float32), 'edge_attr_sh': jax.random.normal(ks[2], (E, 4), jnp.float32), 'edge_src': jax.random.randint(ks[3], (E,), 0, N), 'edge_dst': jax.random.randint(ks[4], (E,), 0, N), 'Wfc1': jax.random.normal(ks[5], (FC_IN, FC_H), jnp.float32), 'Wfc2': jax.random.normal(ks[6], (FC_H, WNUM), jnp.float32), 'Wsc0': jax.random.normal(ks[7], (MUL0, MUL0), jnp.float32), 'Wsc1': jax.random.normal(ks[8], (MUL1, MUL1), jnp.float32), 'Wl1_0': jax.random.normal(ks[9], (MUL0, MUL0), jnp.float32), 'Wl1_1': jax.random.normal(ks[10], (MUL1, MUL1), jnp.float32), 'Wl2_s': jax.random.normal(ks[11], (MUL0 + MUL1, MUL0), jnp.float32), 'Wl2_v': jax.random.normal(ks[12], (MUL0 + MUL1, MUL1), jnp.float32), 'Wa': 0.1 * jax.random.normal(ks[13], (MUL0 + MUL1, 1), jnp.float32)}
    _L0_gnn_all = _L0_gnn_setup()
    _L0_gnn_in = {k: v for k, v in _L0_gnn_all.items() if k in ('Wfc1', 'Wfc2', 'Wsc0', 'Wsc1', 'Wl1_0', 'Wl1_1', 'Wl2_s', 'Wl2_v', 'Wa')}
    del _L0_gnn_all

    def _L1_gnn_setup():
        import jax, jax.numpy as jnp
        import numpy as np
        N_NODES = 6250
        N_EDGES = 100000
        MUL0, MUL1 = (64, 32)
        N_BASIS, N_RADIAL = (10, 100)
        W_NUMEL = 192
        NUM_NEIGHBORS = 16.0
        INV_SQRT3 = np.float32(1.0 / np.sqrt(3.0))
        RELU_GAIN = np.float32(np.sqrt(2.0))
        FAN_L2 = np.float32(np.sqrt(MUL0 + MUL1))

        def _fctp_scalar_attr(x0, x1, a, W0, W1):
            o0 = x0 @ W0 * a * (1.0 / np.sqrt(W0.shape[0]))
            o1 = jnp.einsum('nud,uw->nwd', x1, W1) * a[..., None] * (1.0 / np.sqrt(W1.shape[0]))
            return (o0, o1)
        key = jax.random.key(seed)
        ks = jax.random.split(key, 16)
        return {'node_input': jax.random.normal(ks[0], (N_NODES, MUL0 + 3 * MUL1), jnp.float32), 'node_attr': jnp.ones((N_NODES, 1), jnp.float32), 'edge_attr': jax.random.normal(ks[1], (N_EDGES, 4), jnp.float32), 'edge_length_embedded': jax.random.uniform(ks[2], (N_EDGES, N_BASIS), dtype=jnp.float32), 'W_si0': jax.random.normal(ks[3], (MUL0, MUL0), jnp.float32), 'W_si1': jax.random.normal(ks[4], (MUL1, MUL1), jnp.float32), 'W_l1_0': jax.random.normal(ks[5], (MUL0, MUL0), jnp.float32), 'W_l1_1': jax.random.normal(ks[6], (MUL1, MUL1), jnp.float32), 'W_l2_00': jax.random.normal(ks[7], (MUL0, MUL0), jnp.float32), 'W_l2_10': jax.random.normal(ks[8], (MUL1, MUL0), jnp.float32), 'W_l2_01': jax.random.normal(ks[9], (MUL0, MUL1), jnp.float32), 'W_l2_11': jax.random.normal(ks[10], (MUL1, MUL1), jnp.float32), 'W_fc1': jax.random.normal(ks[11], (N_BASIS, N_RADIAL), jnp.float32), 'W_fc2': jax.random.normal(ks[12], (N_RADIAL, W_NUMEL), jnp.float32), 'edge_src': jax.random.randint(ks[13], (N_EDGES,), 0, N_NODES), 'edge_dst': jax.random.randint(ks[14], (N_EDGES,), 0, N_NODES)}
    _L1_gnn_all = _L1_gnn_setup()
    _L1_gnn_in = {k: v for k, v in _L1_gnn_all.items() if k in ('W_si0', 'W_si1', 'W_l1_0', 'W_l1_1', 'W_l2_00', 'W_l2_10', 'W_l2_01', 'W_l2_11', 'W_fc1', 'W_fc2')}
    del _L1_gnn_all
    return {'x': x, 'src': src, 'dst': dst, 'edge_attr_10': edge_attr_10, 'edge_attr_16': edge_attr_16, 'edge_attr_4': edge_attr_4, 'node_vec1': node_vec1, 'L0_gnn_Wfc1': _L0_gnn_in['Wfc1'], 'L0_gnn_Wfc2': _L0_gnn_in['Wfc2'], 'L0_gnn_Wsc0': _L0_gnn_in['Wsc0'], 'L0_gnn_Wsc1': _L0_gnn_in['Wsc1'], 'L0_gnn_Wl1_0': _L0_gnn_in['Wl1_0'], 'L0_gnn_Wl1_1': _L0_gnn_in['Wl1_1'], 'L0_gnn_Wl2_s': _L0_gnn_in['Wl2_s'], 'L0_gnn_Wl2_v': _L0_gnn_in['Wl2_v'], 'L0_gnn_Wa': _L0_gnn_in['Wa'], 'L1_gnn_W_si0': _L1_gnn_in['W_si0'], 'L1_gnn_W_si1': _L1_gnn_in['W_si1'], 'L1_gnn_W_l1_0': _L1_gnn_in['W_l1_0'], 'L1_gnn_W_l1_1': _L1_gnn_in['W_l1_1'], 'L1_gnn_W_l2_00': _L1_gnn_in['W_l2_00'], 'L1_gnn_W_l2_10': _L1_gnn_in['W_l2_10'], 'L1_gnn_W_l2_01': _L1_gnn_in['W_l2_01'], 'L1_gnn_W_l2_11': _L1_gnn_in['W_l2_11'], 'L1_gnn_W_fc1': _L1_gnn_in['W_fc1'], 'L1_gnn_W_fc2': _L1_gnn_in['W_fc2']}

def reference(x, src, dst, edge_attr_10, edge_attr_16, edge_attr_4, node_vec1, L0_gnn_Wfc1, L0_gnn_Wfc2, L0_gnn_Wsc0, L0_gnn_Wsc1, L0_gnn_Wl1_0, L0_gnn_Wl1_1, L0_gnn_Wl2_s, L0_gnn_Wl2_v, L0_gnn_Wa, L1_gnn_W_si0, L1_gnn_W_si1, L1_gnn_W_l1_0, L1_gnn_W_l1_1, L1_gnn_W_l2_00, L1_gnn_W_l2_10, L1_gnn_W_l2_01, L1_gnn_W_l2_11, L1_gnn_W_fc1, L1_gnn_W_fc2):
    import jax
    import jax.numpy as jnp

    def _L0_gnn_ref(x, node_attr, edge_scalars, edge_attr_sh, edge_src, edge_dst, Wfc1, Wfc2, Wsc0, Wsc1, Wl1_0, Wl1_1, Wl2_s, Wl2_v, Wa):
        import jax, jax.numpy as jnp
        import numpy as np
        N = 2500
        E = 40000
        MUL0 = 64
        MUL1 = 32
        FC_IN = 16
        FC_H = 64
        WNUM = 192
        n = x.shape[0]
        x0 = x[:, :MUL0]
        x1 = x[:, MUL0:].reshape(n, MUL1, 3)
        a = node_attr
        h = jax.nn.silu(edge_scalars @ (Wfc1 / jnp.sqrt(jnp.float32(FC_IN))))
        w = h @ (Wfc2 / jnp.sqrt(jnp.float32(FC_H)))
        w0 = w[:, :64]
        w1 = w[:, 64:128]
        w2 = w[:, 128:160]
        w3 = w[:, 160:192]
        inv8 = 1.0 / jnp.sqrt(jnp.float32(MUL0))
        inv32 = 1.0 / jnp.sqrt(jnp.float32(MUL1))
        sc = jnp.concatenate([x0 @ Wsc0 * a * inv8, (jnp.einsum('num,uv->nvm', x1, Wsc1) * a[..., None] * inv32).reshape(n, 3 * MUL1)], axis=1)
        f0 = x0 @ Wl1_0 * a * inv8
        f1 = jnp.einsum('num,uv->nvm', x1, Wl1_1) * a[..., None] * inv32
        e0 = f0[edge_src]
        e1 = f1[edge_src]
        sh0 = edge_attr_sh[:, :1]
        sh1 = edge_attr_sh[:, 1:4]
        mid0 = w0 * e0 * sh0
        mid1 = w3 * jnp.einsum('eum,em->eu', e1, sh1) / jnp.sqrt(3.0)
        mid2 = w1[:, :, None] * e0[:, :, None] * sh1[:, None, :]
        mid3 = w2[:, :, None] * e1 * sh0[:, :, None]
        cnt = jnp.clip(jax.ops.segment_sum(jnp.ones(edge_dst.shape, x.dtype), edge_dst, num_segments=n), 1.0)

        def smean(v):
            s = jax.ops.segment_sum(v, edge_dst, num_segments=n)
            return s / cnt.reshape((n,) + (1,) * (v.ndim - 1))
        n0, n1 = (smean(mid0), smean(mid1))
        n2, n3 = (smean(mid2), smean(mid3))
        scal = jnp.concatenate([n0, n1], axis=1)
        vec = jnp.concatenate([n2, n3], axis=1)
        inv96 = 1.0 / jnp.sqrt(jnp.float32(MUL0 + MUL1))
        alpha = scal @ Wa * a * inv96
        out_s = scal @ Wl2_s * a * inv96
        out_v = jnp.einsum('num,uv->nvm', vec, Wl2_v) * a[..., None] * inv96
        conv = jnp.concatenate([out_s, out_v.reshape(n, 3 * MUL1)], axis=1)
        return sc + alpha * conv

    def _L1_gnn_ref(node_input, node_attr, edge_src, edge_dst, edge_attr, edge_length_embedded, W_si0, W_si1, W_l1_0, W_l1_1, W_l2_00, W_l2_10, W_l2_01, W_l2_11, W_fc1, W_fc2):
        import jax, jax.numpy as jnp
        import numpy as np
        N_NODES = 6250
        N_EDGES = 100000
        MUL0, MUL1 = (64, 32)
        N_BASIS, N_RADIAL = (10, 100)
        W_NUMEL = 192
        NUM_NEIGHBORS = 16.0
        INV_SQRT3 = np.float32(1.0 / np.sqrt(3.0))
        RELU_GAIN = np.float32(np.sqrt(2.0))
        FAN_L2 = np.float32(np.sqrt(MUL0 + MUL1))

        def _fctp_scalar_attr(x0, x1, a, W0, W1):
            o0 = x0 @ W0 * a * (1.0 / np.sqrt(W0.shape[0]))
            o1 = jnp.einsum('nud,uw->nwd', x1, W1) * a[..., None] * (1.0 / np.sqrt(W1.shape[0]))
            return (o0, o1)
        N = node_input.shape[0]
        x0 = node_input[:, :MUL0]
        x1 = node_input[:, MUL0:].reshape(N, MUL1, 3)
        a = node_attr
        h = jax.nn.relu(edge_length_embedded @ W_fc1 * (1.0 / np.sqrt(N_BASIS))) * RELU_GAIN
        w = h @ W_fc2 * (1.0 / np.sqrt(N_RADIAL))
        w0, w1, w2, w3 = (w[:, :64], w[:, 64:128], w[:, 128:160], w[:, 160:192])
        si0, si1 = _fctp_scalar_attr(x0, x1, a, W_si0, W_si1)
        l0, l1 = _fctp_scalar_attr(x0, x1, a, W_l1_0, W_l1_1)
        y0 = l0[edge_src]
        y1 = l1[edge_src]
        e0 = edge_attr[:, :1]
        e1 = edge_attr[:, 1:4]
        m0 = w0 * y0 * e0
        m1 = (w1 * y0)[:, :, None] * e1[:, None, :]
        m2 = (w2 * e0)[:, :, None] * y1
        m3 = w3 * jnp.einsum('eud,ed->eu', y1, e1) * INV_SQRT3
        inv = np.float32(1.0 / np.sqrt(NUM_NEIGHBORS))
        s0 = jax.ops.segment_sum(m0, edge_dst, num_segments=N) * inv
        s1 = jax.ops.segment_sum(m1, edge_dst, num_segments=N) * inv
        s2 = jax.ops.segment_sum(m2, edge_dst, num_segments=N) * inv
        s3 = jax.ops.segment_sum(m3, edge_dst, num_segments=N) * inv
        o0 = (s0 @ W_l2_00 + s3 @ W_l2_10) * a / FAN_L2
        o1 = (jnp.einsum('nud,uw->nwd', s1, W_l2_01) + jnp.einsum('nud,uw->nwd', s2, W_l2_11)) * a[..., None] / FAN_L2
        out0 = si0 + 0.5 * o0
        out1 = si1 + 0.5 * o1
        return jnp.concatenate([out0, out1.reshape(N, 3 * MUL1)], axis=1)
    x = _layernorm(x + _L0_gnn_ref(x, node_vec1, edge_attr_16, edge_attr_4, src, dst, L0_gnn_Wfc1, L0_gnn_Wfc2, L0_gnn_Wsc0, L0_gnn_Wsc1, L0_gnn_Wl1_0, L0_gnn_Wl1_1, L0_gnn_Wl2_s, L0_gnn_Wl2_v, L0_gnn_Wa), axis=-1)
    x = _layernorm(x + _L1_gnn_ref(x, node_vec1, src, dst, edge_attr_4, edge_attr_10, L1_gnn_W_si0, L1_gnn_W_si1, L1_gnn_W_l1_0, L1_gnn_W_l1_1, L1_gnn_W_l2_00, L1_gnn_W_l2_10, L1_gnn_W_l2_01, L1_gnn_W_l2_11, L1_gnn_W_fc1, L1_gnn_W_fc2), axis=-1)
    return x

_drawn_inputs = setup_inputs


def setup_inputs(seed=0):
    import zlib

    import numpy as np

    out = dict(_drawn_inputs(seed))
    spreads = {}
    factors = {'edge_attr_16': 8.0,
     'L0_gnn_Wfc1': 8.0,
     'L0_gnn_Wfc2': 8.0,
     'L0_gnn_Wl1_0': 8.0,
     'L0_gnn_Wl1_1': 8.0,
     'L0_gnn_Wl2_s': 8.0,
     'L0_gnn_Wl2_v': 8.0,
     'L0_gnn_Wa': 8.0}
    for name, (base, spread) in spreads.items():
        noise = np.random.default_rng([zlib.crc32(name.encode()), seed]).standard_normal(out[name].shape)
        drawn = base * np.exp(spread * noise) if base else spread * noise
        out[name] = jnp.asarray(drawn.astype(out[name].dtype))
    for name, factor in factors.items():
        out[name] = (out[name] * factor).astype(out[name].dtype)
    return out
```

```python
import math
from contextlib import ExitStack

import concourse.bass as bass
from concourse import mybir

P = 128
MUL0, MUL1, VEC = 64, 32, 3
FEAT = MUL0 + VEC * MUL1
WNUM = 2 * MUL0 + 2 * MUL1
PROD = 2 * MUL0 + 2 * VEC * MUL1
TILES = 4
CHUNK = TILES * P
SLOTS = 4
WIN = 32
SPH = 4
BLOCKS = 5
BANK = 512
LN_EPS = 1e-5


def build(nc, d, n_nodes, n_chunks, n_ntiles):
    f32, i32 = mybir.dt.float32, mybir.dt.int32
    ALU, ACT = mybir.AluOpType, mybir.ActivationFunctionType
    AX = mybir.AxisListType
    n_rows = n_ntiles * P
    assert n_chunks % SLOTS == 0 and n_ntiles % 2 == 0 and n_rows >= n_nodes + 1 + WIN
    n_iters = n_chunks // SLOTS
    K1 = (16, 10)
    H = (64, 100)
    h_func = (ACT.Silu, ACT.Relu)
    h_scale = (1.0 / math.sqrt(K1[0]), math.sqrt(2.0) / math.sqrt(K1[1]))
    fan = math.sqrt(MUL0 + MUL1)
    conv_scale = (1.0 / math.sqrt(H[0]) / fan, 0.5 / math.sqrt(16.0) / math.sqrt(H[1]) / fan)
    ALPHA, COUNT = FEAT, FEAT + 1

    with ExitStack() as ctx:
        def sb(name, shape, dt=f32):
            return ctx.enter_context(nc.sbuf_tensor(name, shape, dt))

        def sem(name):
            return ctx.enter_context(nc.semaphore(name))

        acc = sb("acc", [P, BLOCKS, n_rows])
        first_i = sb("first_i", [P, n_chunks], i32)
        first_f = sb("first_f", [P, n_chunks])
        dst_i = sb("dst_i", [P, n_chunks * TILES], i32)
        dst_rel = sb("dst_rel", [P, n_chunks * TILES])
        node_a = sb("node_a", [P, n_ntiles])
        iota_i = sb("iota_i", [P, WIN], i32)
        iota = sb("iota", [P, WIN])
        row_i = sb("row_i", [P, P], i32)
        ident = sb("ident", [P, P])
        ones = sb("ones", [P, P])
        zeros = sb("zeros", [P, BLOCKS, P])
        eps = sb("eps", [P, 1])
        fc1w = [sb(f"fc1w{l}", [P, H[l]]) for l in range(2)]
        fc2w = [sb(f"fc2w{l}", [H[l], WNUM]) for l in range(2)]
        nodew = [sb(f"nodew{l}", [VEC * MUL1, 2, FEAT]) for l in range(2)]
        convw = [sb(f"convw{l}", [P, 2, FEAT + 2]) for l in range(2)]
        attr = sb("attr", [P, CHUNK])
        src = sb("src", [P, SLOTS, TILES], i32)
        sph = sb("sph", [P, SLOTS, TILES, SPH])
        rows = sb("rows", [P, SLOTS, TILES, FEAT])
        hidden = sb("hidden", [P, 2, CHUNK])
        hot = sb("hot", [P, 2, TILES, WIN])
        hot_sum = sb("hot_sum", [P, 2, WIN])
        hot_sph = sb("hot_sph", [P, 2, TILES, SPH, WIN])
        prod = sb("prod", [P, 2, TILES, PROD])
        x_t = sb("x_t", [VEC * MUL1, 2, 2, P])
        x_row = sb("x_row", [P, 2, FEAT])
        tab_out = sb("tab_out", [P, 2, FEAT])
        res_out = sb("res_out", [P, 2, FEAT])
        res_in = sb("res_in", [P, 2, FEAT])
        sums = sb("sums", [P, 2, BLOCKS, P])
        mixed = sb("mixed", [P, 2, FEAT])
        small = sb("small", [P, 2, 16])

        bank = [ctx.enter_context(nc.psum_tensor(f"bank{b}", [P, BANK], f32)) for b in range(8)]
        hid_ps, w_ps, agg_ps = bank[0:2], bank[2:6], bank[6:8]
        conv_ps, trans_ps, tab_ps, self_ps = bank[0:2], bank[2:4], bank[4:6], bank[6:8]

        index_in, weights_zeroed, weights_in = sem("index_in"), sem("weights_zeroed"), sem("weights_in")
        weights_ready = sem("weights_ready")
        iota_made, consts_made, acc_zeroed = sem("iota_made"), sem("consts_made"), sem("acc_zeroed")
        prep_step = sem("prep_step")
        attr_in = [sem(f"attr_in{k}") for k in range(SLOTS)]
        src_in = [sem(f"src_in{k}") for k in range(SLOTS)]
        sph_in = [sem(f"sph_in{k}") for k in range(SLOTS)]
        rows_in = [sem(f"rows_in{k}") for k in range(SLOTS)]
        fc1_done, hidden_ready = sem("fc1_done"), sem("hidden_ready")
        w_ready, prod_done = sem("w_ready"), sem("prod_done")
        hot_made, hot_ready = sem("hot_made"), sem("hot_ready")
        agg_done, acc_added = sem("agg_done"), sem("acc_added")
        x_in = [sem(f"x_in{j}") for j in range(2)]
        res_in_sem = [sem(f"res_in_sem{j}") for j in range(2)]
        tab_stored = [sem(f"tab_stored{j}") for j in range(2)]
        row_stored = [sem(f"row_stored{j}") for j in range(2)]
        node_mm, tab_ready, res_ready = sem("node_mm"), sem("tab_ready"), sem("res_ready")
        sums_staged, conv_done, stats_done = sem("sums_staged"), sem("conv_done"), sem("stats_done")
        std_done, rstd_made, normed = sem("std_done"), sem("rstd_made"), sem("normed")
        transposed, xt_copied, mix_step = sem("transposed"), sem("xt_copied"), sem("mix_step")
        turn = {e: sem(f"turn_{e}") for e in ("sp", "pool", "act", "dve", "pe")}

        def reached(n, least):
            return not isinstance(n, int) or n >= least

        def in_range(n, count):
            return not isinstance(n, int) or 0 <= n < count

        def chunk_no(l, c):
            return l * n_chunks + c

        def slot_loads(g, k, each=16):
            return (each // SLOTS) * (g - k) + each

        def tile_no(phase, n):
            return phase * n_ntiles + n

        def stores_before(number, j):
            return 8 * (number - j)

        def over_chunks(eng, step):
            for k in range(SLOTS):
                step(k, k)
            with eng.Fori(1, n_iters) as i:
                for k in range(SLOTS):
                    step(i * SLOTS + k, k)

        def over_tiles(eng, step, lag):
            for n in range(4):
                step(n, n % 2)
            with eng.Fori(2, n_ntiles // 2) as i:
                for j in range(2):
                    step(i * 2 + j, j)
            for n in range(n_ntiles, n_ntiles + lag):
                step(n, n % 2)

        def held(eng, value):
            return value if isinstance(value, int) else eng.snap(value)

        def weight_loads(l):
            w = {k: d[f"L{l}_{k}"] for k in ("fc1", "fc2", "t0", "t1", "s0", "s1", "a", "b", "c", "dd")}
            out = [(fc1w[l][32 * k:32 * k + K1[l], :], w["fc1"]) for k in range(SLOTS)]
            out.append((fc2w[l][:, :], w["fc2"]))
            for s, (w0, w1) in enumerate((("t0", "t1"), ("s0", "s1"))):
                out.append((nodew[l][0:MUL0, s, 0:MUL0], w[w0]))
                for m in range(VEC):
                    out.append((nodew[l][32 * m:32 * m + 32, s, MUL0 + 32 * m:MUL0 + 32 * m + 32], w[w1]))
            for m in range(VEC):
                out.append((convw[l][32 * m:32 * m + 32, 0, MUL0 + 32 * m:MUL0 + 32 * m + 32], w["c"]))
            out.append((convw[l][96:128, 0, 0:MUL0], w["dd"]))
            out.append((convw[l][0:MUL0, 1, 0:MUL0], w["a"]))
            out.append((convw[l][MUL0:P, 1, MUL0:MUL0 + MUL1], w["b"]))
            if l == 0:
                out.append((convw[l][96:128, 0, ALPHA:ALPHA + 1], d["L0_alpha"][MUL0:MUL0 + MUL1, :]))
                out.append((convw[l][0:MUL0, 1, ALPHA:ALPHA + 1], d["L0_alpha"][0:MUL0, :]))
            return out
        loads = weight_loads(0), weight_loads(1)
        n_weight_loads = len(loads[0]) + len(loads[1])

        block = ctx.enter_context(nc.Block())

        @block.sync
        def _(sp):
            sp.dma_start(dst_i[:, :], d["dst"]).then_inc(index_in, 16)
            sp.dma_start(first_i[:, :], d["first"].partition_broadcast(P)).then_inc(index_in, 16)
            sp.dma_start(node_a[:, :], d["node_a"]).then_inc(index_in, 16)
            sp.wait_ge(weights_zeroed, 4)
            for dst, source in loads[0]:
                sp.dma_start(dst, source).then_inc(weights_in, 16)

            def load_x(n, j):
                at = held(sp, n * P)
                if reached(n, 2):
                    sp.wait_ge(res_ready, n - 1)
                    sp.sem_inc(turn["sp"])
                cols = bass.ds(at, P)
                sp.dma_start(x_t[0:MUL0, j, 0, :], d["xt0"][:, cols]).then_inc(x_in[j], 16)
                sp.dma_start(x_t[:, j, 1, :], d["xt1"][:, cols]).then_inc(x_in[j], 16)
                sp.dma_start(x_row[:, j, :], d["x"][cols, :]).then_inc(x_in[j], 16)
            over_tiles(sp, load_x, 0)

            def load_edges(l, c, k):
                g = chunk_no(l, c)
                at = held(sp, c)
                if reached(g, SLOTS):
                    sp.wait_ge(fc1_done, g - 3)
                    sp.sem_inc(turn["sp"])
                sp.dma_start(attr[32 * k:32 * k + K1[l], :], d[f"attr{l}"][bass.ds(at, 1), :, :]
                             .rearrange("o k e -> (o k) e")).then_inc(attr_in[k], 16)
                if reached(g, SLOTS):
                    sp.wait_ge(rows_in[k], slot_loads(g - SLOTS, k, 16 * TILES))
                    sp.sem_inc(turn["sp"])
                sp.dma_start(src[:, k, :], d["src"][bass.ds(at, 1), :, :]
                             .rearrange("o p t -> (o p) t")).then_inc(src_in[k], 16)
                if reached(g, SLOTS):
                    sp.wait_ge(hot_ready, g - 3)
                    sp.sem_inc(turn["sp"])
                sp.dma_start(sph[:, k, :, :].rearrange("p t m -> p (t m)"), d["sph"][bass.ds(at, 1), :, :]
                             .rearrange("o p e -> (o p) e")).then_inc(sph_in[k], 16)

            for l in range(2):
                over_chunks(sp, lambda c, k: load_edges(l, c, k))
                phase = l + 1
                for j in range(2):
                    sp.wait_ge(row_stored[j], stores_before(tile_no(phase, j), j))

                def load_res(n, j):
                    at = held(sp, n * P)
                    if reached(tile_no(l, n), 2):
                        sp.wait_ge(stats_done, tile_no(l, n) - 1)
                        sp.sem_inc(turn["sp"])
                    sp.dma_start(res_in[:, j, :], d[f"resid{l}"][bass.ds(at, P), :]).then_inc(res_in_sem[j], 16)
                over_tiles(sp, load_res, 0)

        @block.gpsimd
        def _(pool):
            nc.gpsimd.iota(iota_i[:, :], pattern=[[1, WIN]], base=0, channel_multiplier=0).then_inc(iota_made, 1)
            nc.gpsimd.iota(row_i[:, :], pattern=[[1, P]], base=0, channel_multiplier=-1).then_inc(iota_made, 1)
            nc.gpsimd.memset(ones[:, :], 1.0).then_inc(consts_made, 1)
            nc.gpsimd.memset(zeros[:, :, :], 0.0).then_inc(consts_made, 1)
            nc.gpsimd.memset(acc[:, :, :], 0.0).then_inc(acc_zeroed, 1)

            def store_rows(phase, n, j):
                at = held(pool, n * P)
                rows_at = bass.ds(at, P)
                pool.wait_ge(tab_ready, tile_no(phase, n) + 1)
                pool.sem_inc(turn["pool"])
                pool.dma_start(d[f"table{phase}"][rows_at, :], tab_out[:, j, :]).then_inc(tab_stored[j], 16)
                pool.wait_ge(res_ready, tile_no(phase, n) + 1)
                pool.sem_inc(turn["pool"])
                pool.dma_start(d[f"resid{phase}"][rows_at, :], res_out[:, j, :]).then_inc(row_stored[j], 16)
            over_tiles(pool, lambda n, j: store_rows(0, n, j), 0)

            def gather(l, c, k):
                g = chunk_no(l, c)
                if reached(g, SLOTS):
                    pool.wait_ge(prod_done, 2 * (g - 3))
                pool.wait_ge(src_in[k], slot_loads(g, k))
                pool.sem_inc(turn["pool"])
                for t in range(TILES):
                    nc.gpsimd.indirect_dma_start(
                        out=rows[:, k, t, :], out_offset=None, in_=d[f"table{l}"],
                        in_offset=bass.IndirectOffsetOnAxis(ap=src[:, k, t:t + 1], axis=0)).then_inc(rows_in[k], 16)

            for l in range(2):
                for j in range(2):
                    pool.wait_ge(tab_stored[j], stores_before(tile_no(l + 1, j), j))
                over_chunks(pool, lambda c, k: gather(l, c, k))
                if l == 0:
                    pool.wait_ge(consts_made, 2)

                    def between(n, j):
                        if in_range(n - 3, n_ntiles):
                            store_rows(1, n - 3, 1 - j)
                        if in_range(n, n_ntiles):
                            at = held(pool, n * P)
                            pool.wait_ge(sums_staged, n + 1)
                            pool.sem_inc(turn["pool"])
                            nc.gpsimd.tensor_copy(acc[:, :, bass.ds(at, P)], zeros[:, :, :]).then_inc(acc_zeroed, 1)
                    over_tiles(pool, between, 3)

            def store_out(n, j):
                at = held(pool, n * P)
                pool.wait_ge(normed, tile_no(1, n) + 1)
                pool.sem_inc(turn["pool"])
                pool.dma_start(d["out"][bass.ds(at, P), :], x_row[:, j, :]).then_inc(row_stored[j], 16)
            over_tiles(pool, store_out, 0)
            for j in range(2):
                pool.wait_ge(row_stored[j], stores_before(tile_no(3, j), j))
                pool.wait_ge(tab_stored[j], stores_before(tile_no(2, j), j))

        @block.scalar
        def _(act):
            act.wait_ge(weights_zeroed, 4)
            for dst, source in loads[1]:
                act.dma_start(dst, source).then_inc(weights_in, 16)
            act.wait_ge(index_in, 48)

            def table_out(phase, n, j):
                number, at = tile_no(phase, n), held(act, n)
                act.wait_ge(node_mm, number + 1)
                if reached(number, 2):
                    act.wait_ge(tab_stored[j], stores_before(number, j))
                    act.sem_inc(turn["act"])
                nc.scalar.activation(tab_out[:, j, :], tab_ps[j][:, 0:FEAT], ACT.Copy,
                                     scale=node_a[:, bass.ds(at, 1)]).then_inc(tab_ready, 1)
            over_tiles(act, lambda n, j: table_out(0, n, j), 0)

            def hidden_act(l, c, k):
                g = chunk_no(l, c)
                act.wait_ge(fc1_done, g + 1)
                if reached(g, 2):
                    act.wait_ge(w_ready, 2 * (g - 1))
                nc.scalar.activation(hidden[0:H[l], k % 2, :], hid_ps[k % 2][0:H[l], :], h_func[l],
                                     scale=h_scale[l]).then_inc(hidden_ready, 1)

            def node_step(l, n, j):
                blocks = BLOCKS - l
                if in_range(n, n_ntiles):
                    at, number = held(act, n * P), tile_no(l, n)
                    if reached(number, 2):
                        act.wait_ge(conv_done, number - 1)
                        act.sem_inc(turn["act"])
                    nc.scalar.copy(sums[:, j, 0:blocks, :],
                                   acc[:, 0:blocks, bass.ds(at, P)]).then_inc(sums_staged, 1)
                if in_range(n - 1, n_ntiles):
                    act.wait_ge(stats_done, tile_no(l, n - 1) + 1)
                    nc.scalar.activation(small[:, 1 - j, 12:13], small[:, 1 - j, 11:12], ACT.Sqrt,
                                         bias=eps[:, 0:1]).then_inc(std_done, 1)
                if l == 0 and in_range(n - 2, n_ntiles):
                    act.wait_ge(transposed, n - 1)
                    if reached(n - 2, 2):
                        act.wait_ge(node_mm, tile_no(1, n - 4) + 1)
                        act.sem_inc(turn["act"])
                    nc.scalar.copy(x_t[0:MUL0, j, 0, :], trans_ps[j][0:MUL0, 0:P])
                    nc.scalar.copy(x_t[:, j, 1, :], trans_ps[j][0:VEC * MUL1, P:2 * P]).then_inc(xt_copied, 1)
                if l == 0 and in_range(n - 3, n_ntiles):
                    table_out(1, n - 3, 1 - j)

            act.wait_ge(consts_made, 3)
            for l in range(2):
                over_chunks(act, lambda c, k: hidden_act(l, c, k))
                act.wait_ge(acc_added, chunk_no(l + 1, 0))
                over_tiles(act, lambda n, j: node_step(l, n, j), 3 if l == 0 else 1)

        @block.vector
        def _(dve):
            steps = [0]

            def own(ins):
                steps[0] += 1
                ins.then_inc(prep_step, 1)
                dve.wait_ge(prep_step, steps[0])

            for l in range(2):
                nc.vector.memset(nodew[l][:, :, :], 0.0).then_inc(weights_zeroed, 1)
                nc.vector.memset(convw[l][:, :, :], 0.0).then_inc(weights_zeroed, 1)
            nc.vector.memset(eps[:, :], LN_EPS).then_inc(consts_made, 1)
            dve.wait_ge(iota_made, 2)
            nc.vector.tensor_copy(iota[:, :], iota_i[:, :])
            own(nc.vector.tensor_scalar(ident[:, :], row_i[:, :], 0.0, None, ALU.is_equal))
            dve.wait_ge(index_in, 48)
            nc.vector.tensor_copy(dst_rel[:, :], dst_i[:, :])
            own(nc.vector.tensor_copy(first_f[:, :], first_i[:, :]))
            by_chunk = dst_rel[:, :].rearrange("p (c t) -> p c t", t=TILES)
            own(nc.vector.tensor_tensor(by_chunk, by_chunk, first_f[:, :].unsqueeze(2)
                                        .broadcast_to([P, n_chunks, TILES]), ALU.subtract))
            dve.wait_ge(weights_in, 16 * n_weight_loads)
            for l in range(2):
                nc.vector.tensor_scalar(nodew[l][:, :, 0:MUL0], nodew[l][:, :, 0:MUL0],
                                        1.0 / math.sqrt(MUL0), None, ALU.mult)
                nc.vector.tensor_scalar(nodew[l][:, :, MUL0:FEAT], nodew[l][:, :, MUL0:FEAT],
                                        1.0 / math.sqrt(MUL1), None, ALU.mult)
                own(nc.vector.tensor_scalar(convw[l][:, :, :], convw[l][:, :, :], conv_scale[l], None, ALU.mult))
                third = 1.0 / math.sqrt(VEC)
                own(nc.vector.tensor_scalar(convw[l][96:128, 0, 0:MUL0], convw[l][96:128, 0, 0:MUL0],
                                            third, None, ALU.mult))
            own(nc.vector.tensor_scalar(convw[0][96:128, 0, ALPHA:ALPHA + 1], convw[0][96:128, 0, ALPHA:ALPHA + 1],
                                        third, None, ALU.mult))
            nc.vector.tensor_copy(small[:, 0, 0:1], eps[:, :]).then_inc(weights_ready, 1)

            def resid_out(phase, n, j):
                number, at = tile_no(phase, n), held(dve, n)
                dve.wait_ge(node_mm, number + 1)
                if reached(number, 2):
                    dve.wait_ge(row_stored[j], stores_before(number, j))
                    dve.sem_inc(turn["dve"])
                nc.vector.scalar_tensor_tensor(out=res_out[:, j, :], in0=self_ps[j][:, 0:FEAT],
                                               scalar=node_a[:, bass.ds(at, 1)], in1=x_row[:, j, :],
                                               op0=ALU.mult, op1=ALU.add).then_inc(res_ready, 1)

            def pre_step(n, j):
                dve.wait_ge(x_in[j], stores_before(n, j) * 3 + 48)
                resid_out(0, n, j)
            over_tiles(dve, pre_step, 0)

            def windows(l, c, k):
                g, at = chunk_no(l, c), held(dve, c * TILES)
                if reached(g, 2):
                    dve.wait_ge(agg_done, g - 1)
                    dve.sem_inc(turn["dve"])
                nc.vector.tensor_tensor(
                    hot[:, k % 2, :, :], iota[:, :].unsqueeze(1).broadcast_to([P, TILES, WIN]),
                    dst_rel[:, bass.ds(at, TILES)].unsqueeze(2).broadcast_to([P, TILES, WIN]),
                    ALU.is_equal).then_inc(hot_made, 1)
                dve.wait_ge(sph_in[k], slot_loads(g, k))
                dve.wait_ge(hot_made, g + 1)
                if l == 0:
                    nc.vector.tensor_reduce(hot_sum[:, k % 2, :], hot[:, k % 2, :, :].rearrange("p t w -> p w t"),
                                            AX.X, ALU.add)
                nc.vector.tensor_tensor(
                    hot_sph[:, k % 2, :, :, :], hot[:, k % 2, :, :].unsqueeze(2).broadcast_to([P, TILES, SPH, WIN]),
                    sph[:, k, :, :].unsqueeze(3).broadcast_to([P, TILES, SPH, WIN]),
                    ALU.mult).then_inc(hot_ready, 1)

            def products(l, c, k):
                g = chunk_no(l, c)
                dve.wait_ge(rows_in[k], slot_loads(g, k, 16 * TILES))
                for q in range(2):
                    w = w_ps[2 * (k % 2) + q][:, 0:2 * WNUM].rearrange("p (t n) -> p t n", t=2)
                    out = prod[:, k % 2, 2 * q:2 * q + 2, :]
                    row = rows[:, k, 2 * q:2 * q + 2, :]
                    dve.wait_ge(w_ready, 2 * g + q + 1)
                    nc.vector.tensor_tensor(
                        out[:, :, 0:2 * MUL0].rearrange("p t (s u) -> p t s u", s=2),
                        w[:, :, 0:2 * MUL0].rearrange("p t (s u) -> p t s u", s=2),
                        row[:, :, 0:MUL0].unsqueeze(2).broadcast_to([P, 2, 2, MUL0]), ALU.mult)
                    for s in range(2):
                        at, wat = 2 * MUL0 + s * VEC * MUL1, 2 * MUL0 + s * MUL1
                        last = nc.vector.tensor_tensor(
                            out[:, :, at:at + VEC * MUL1].rearrange("p t (m u) -> p t m u", m=VEC),
                            w[:, :, wat:wat + MUL1].unsqueeze(2).broadcast_to([P, 2, VEC, MUL1]),
                            row[:, :, MUL0:FEAT].rearrange("p t (m u) -> p t m u", m=VEC), ALU.mult)
                    last.then_inc(prod_done, 1)

            def add_sums(l, c, k):
                g = chunk_no(l, c)
                at = dve.value_load(first_i[0:1, bass.ds(c, 1)], min_val=0, max_val=n_nodes)
                nodes, ps = bass.ds(at, WIN), agg_ps[k % 2]
                dve.wait_ge(agg_done, g + 1)
                if reached(g, 1):
                    dve.wait_ge(acc_added, g)
                    dve.sem_inc(turn["dve"])
                nc.vector.tensor_tensor(acc[0:MUL0, 0, nodes], acc[0:MUL0, 0, nodes], ps[0:MUL0, 0:WIN], ALU.add)
                nc.vector.tensor_tensor(acc[MUL0:P, 0:VEC, nodes], acc[MUL0:P, 0:VEC, nodes],
                                        ps[MUL0:P, WIN:SPH * WIN].rearrange("p (m w) -> p m w", m=VEC), ALU.add)
                n = 2 - l
                nc.vector.tensor_tensor(acc[:, VEC:VEC + n, nodes], acc[:, VEC:VEC + n, nodes],
                                        ps[:, SPH * WIN:(SPH + n) * WIN].rearrange("p (b w) -> p b w", b=n),
                                        ALU.add).then_inc(acc_added, 1)

            def mix(l, n, j):
                number, at = tile_no(l, n), held(dve, n)
                done = 6 * number if l == 0 else 6 * n_ntiles + 3 * n
                ps, res = conv_ps[j], res_in[:, j, :]
                dve.wait_ge(res_in_sem[j], stores_before(number, j) + 16)
                dve.wait_ge(conv_done, number + 1)
                s = [small[:, j, i:i + 1] for i in range(16)]
                a = node_a[:, bass.ds(at, 1)]
                count = [0]

                def after(ins):
                    count[0] += 1
                    ins.then_inc(mix_step, 1)
                    dve.wait_ge(mix_step, done + count[0])
                    dve.sem_inc(turn["dve"])
                if l == 0:
                    dve.sem_inc(turn["dve"])
                    after(nc.vector.tensor_scalar(s[0], ps[:, COUNT:COUNT + 1], 1.0, None, ALU.max))
                    after(nc.vector.reciprocal(s[1], s[0]))
                    after(nc.vector.tensor_tensor(s[2], s[1], a, ALU.mult))
                    after(nc.vector.tensor_scalar(s[3], ps[:, ALPHA:ALPHA + 1], s[2], s[2], ALU.mult, ALU.mult))
                else:
                    dve.sem_inc(turn["dve"])
                    after(nc.vector.tensor_copy(s[3], a))
                after(nc.vector.scalar_tensor_tensor(out=mixed[:, j, :], in0=ps[:, 0:FEAT], scalar=s[3], in1=res,
                                                     op0=ALU.mult, op1=ALU.add))
                after(nc.vector.bn_stats(s_stats(j), mixed[:, j, :]))
                nc.vector.bn_aggr(small[:, j, 10:12], s_stats(j)).then_inc(stats_done, 1)

            def s_stats(j):
                return small[:, j, 4:10]

            def norm(l, n, j):
                number = tile_no(l, n)
                dve.wait_ge(std_done, number + 1)
                nc.vector.reciprocal(small[:, j, 13:14], small[:, j, 12:13]).then_inc(rstd_made, 1)
                if l == 0 and reached(n, 2):
                    dve.wait_ge(transposed, n - 1)
                if l == 1:
                    dve.wait_ge(row_stored[j], stores_before(tile_no(2, n), j))
                dve.wait_ge(rstd_made, number + 1)
                dve.sem_inc(turn["dve"])
                nc.vector.tensor_scalar(x_row[:, j, :], mixed[:, j, :], small[:, j, 10:11], small[:, j, 13:14],
                                        ALU.subtract, ALU.mult).then_inc(normed, 1)

            def node_step(l, n, j):
                if l == 0 and in_range(n - 3, n_ntiles):
                    resid_out(1, n - 3, 1 - j)
                if in_range(n, n_ntiles):
                    mix(l, n, j)
                if in_range(n - 1, n_ntiles):
                    norm(l, n - 1, 1 - j)

            dve.wait_ge(acc_zeroed, 1)
            for l in range(2):
                def chunk_step(c, k):
                    windows(l, c, k)
                    if reached(c, 1):
                        add_sums(l, c - 1, (k - 1) % SLOTS)
                    products(l, c, k)
                over_chunks(dve, chunk_step)
                add_sums(l, n_chunks - 1, SLOTS - 1)
                over_tiles(dve, lambda n, j: node_step(l, n, j), 3 if l == 0 else 1)
                if l == 0:
                    dve.wait_ge(acc_zeroed, 1 + n_ntiles)

        @block.tensor
        def _(pe):
            mm = nc.tensor.matmul
            pe.wait_ge(weights_ready, 1)

            def node_maps(phase, n, j):
                number, w = tile_no(phase, n), nodew[phase]
                if reached(number, 2):
                    pe.wait_ge(tab_ready, number - 1)
                    pe.wait_ge(res_ready, number - 1)
                if phase == 0:
                    pe.wait_ge(x_in[j], stores_before(n, j) * 3 + 48)
                else:
                    pe.wait_ge(xt_copied, n + 1)
                for s, ps in enumerate((tab_ps[j], self_ps[j])):
                    mm(ps[:, 0:MUL0], x_t[0:MUL0, j, 0, :], w[0:MUL0, s, 0:MUL0], start=True, stop=True)
                    last = mm(ps[:, MUL0:FEAT], x_t[:, j, 1, :], w[:, s, MUL0:FEAT], start=True, stop=True)
                last.then_inc(node_mm, 1)
            over_tiles(pe, lambda n, j: node_maps(0, n, j), 0)

            def fc1(l, c, k):
                g = chunk_no(l, c)
                if reached(g, 2):
                    pe.wait_ge(hidden_ready, g - 1)
                pe.wait_ge(attr_in[k], slot_loads(g, k))
                at = 32 * k
                mm(hid_ps[k % 2][0:H[l], :], fc1w[l][at:at + K1[l], :], attr[at:at + K1[l], :],
                   start=True, stop=True, tile_position=(at, 0)).then_inc(fc1_done, 1)

            def fc2(l, c, k):
                g = chunk_no(l, c)
                pe.wait_ge(hidden_ready, g + 1)
                for q in range(2):
                    if reached(g, 2):
                        pe.wait_ge(prod_done, 2 * (g - 2) + q + 1)
                    ps = w_ps[2 * (k % 2) + q]
                    for t in range(2):
                        e = (2 * q + t) * P
                        last = mm(ps[:, t * WNUM:(t + 1) * WNUM], hidden[0:H[l], k % 2, e:e + P],
                                  fc2w[l][:, :], start=True, stop=True)
                    last.then_inc(w_ready, 1)

            def sum_edges(l, c, k):
                g, ps = chunk_no(l, c), agg_ps[k % 2]
                if reached(g, 2):
                    pe.wait_ge(acc_added, g - 1)
                pe.wait_ge(hot_ready, g + 1)
                pe.wait_ge(prod_done, 2 * g + 2)
                for t in range(TILES):
                    p, h = prod[:, k % 2, t, :], hot_sph[:, k % 2, t, :, :]
                    mm(ps[:, 0:SPH * WIN], p[:, 0:2 * MUL0], h.rearrange("p m w -> p (m w)"),
                       start=(t == 0), stop=(t == TILES - 1), skip_group_check=True)
                    mm(ps[0:96, SPH * WIN:(SPH + 1) * WIN], p[:, 2 * MUL0:2 * MUL0 + 96], h[:, 0, :],
                       start=False, stop=(t == TILES - 1), skip_group_check=True)
                if l == 0:
                    mm(ps[:, (SPH + 1) * WIN:(SPH + 2) * WIN], ones[:, :], hot_sum[:, k % 2, :],
                       start=False, stop=True, skip_group_check=True)
                for t in range(TILES):
                    p, h = prod[:, k % 2, t, :], hot_sph[:, k % 2, t, :, :]
                    for m in range(VEC):
                        at = 2 * MUL0 + 96 + m * MUL1
                        last = mm(ps[96:128, SPH * WIN:(SPH + 1) * WIN], p[:, at:at + MUL1], h[:, 1 + m, :],
                                  start=False, stop=(t == TILES - 1 and m == VEC - 1), skip_group_check=True,
                                  tile_position=(0, 96))
                last.then_inc(agg_done, 1)

            def conv(l, n, j):
                number, ps, w, cols = tile_no(l, n), conv_ps[j], convw[l], FEAT + 1 - l
                if reached(number, 2):
                    pe.wait_ge(stats_done, number - 1)
                pe.wait_ge(sums_staged, number + 1)
                mm(ps[:, 0:cols], sums[:, j, 3, :], w[:, 0, 0:cols], start=True, stop=False, skip_group_check=True)
                last = mm(ps[:, 0:cols], sums[:, j, 0, :], w[:, 1, 0:cols], start=False, stop=True,
                          skip_group_check=True)
                if l == 0:
                    last = mm(ps[:, COUNT:COUNT + 1], sums[0:32, j, 4, :], ident[0:32, 0:1],
                              start=False, stop=True, skip_group_check=True)
                for m in (1, 2):
                    at = MUL0 + m * MUL1
                    last = mm(ps[:, at:at + MUL1], sums[MUL0:P, j, m, :], w[MUL0:P, 1, MUL0:MUL0 + MUL1],
                              start=False, stop=True, skip_group_check=True)
                last.then_inc(conv_done, 1)

            def transpose(n, j):
                if reached(n, 2):
                    pe.wait_ge(xt_copied, n - 1)
                pe.wait_ge(normed, n + 1)
                pe.sem_inc(turn["pe"])
                nc.tensor.transpose(trans_ps[j][0:MUL0, 0:P], x_row[:, j, 0:MUL0], ident[:, :])
                nc.tensor.transpose(trans_ps[j][0:VEC * MUL1, P:2 * P], x_row[:, j, MUL0:FEAT],
                                    ident[:, :]).then_inc(transposed, 1)

            def node_step(l, n, j):
                if l == 0 and in_range(n - 3, n_ntiles):
                    node_maps(1, n - 3, 1 - j)
                if in_range(n, n_ntiles):
                    conv(l, n, j)
                if l == 0 and in_range(n - 2, n_ntiles):
                    transpose(n - 2, j)

            for l in range(2):
                def chunk_step(c, k):
                    fc1(l, c, k)
                    if reached(c, 1):
                        sum_edges(l, c - 1, (k - 1) % SLOTS)
                    fc2(l, c, k)
                if l == 0:
                    pe.wait_ge(consts_made, 3)
                over_chunks(pe, chunk_step)
                sum_edges(l, n_chunks - 1, SLOTS - 1)
                over_tiles(pe, lambda n, j: node_step(l, n, j), 3 if l == 0 else 0)


def kernel(**inputs):
    import numpy as np
    import concourse.bacc as bacc
    from concourse import mybir as mb
    from concourse.bass_utils import run_bass_kernel_spmd

    a = {k: np.asarray(v) for k, v in inputs.items()}
    n_nodes, n_edges = a["x"].shape[0], a["src"].shape[0]
    n_chunks = -(-n_edges // (CHUNK * SLOTS)) * SLOTS
    n_ntiles = -(-(n_nodes + 1 + WIN) // (2 * P)) * 2
    n_rows, pad = n_ntiles * P, n_chunks * CHUNK - n_edges

    def component_major(x):
        return x.reshape(-1, MUL1, VEC).transpose(0, 2, 1).reshape(-1, VEC * MUL1)

    x = np.zeros((n_rows, FEAT), a["x"].dtype)
    x[:n_nodes, :MUL0] = a["x"][:, :MUL0]
    x[:n_nodes, MUL0:] = component_major(a["x"][:, MUL0:])
    node_a = np.zeros((n_rows, 1), a["node_vec1"].dtype)
    node_a[:n_nodes] = a["node_vec1"]
    src = np.concatenate([a["src"], np.zeros(pad, a["src"].dtype)]).reshape(n_chunks, TILES, P)
    dst = np.concatenate([a["dst"], np.full(pad, n_nodes, a["dst"].dtype)]).reshape(n_chunks, TILES, P)

    def edges(v):
        return np.concatenate([v, np.zeros((pad, v.shape[1]), v.dtype)]).reshape(n_chunks, TILES, P, v.shape[1])
    arrays = {
        "x": x, "xt0": x[:, :MUL0].T, "xt1": x[:, MUL0:].T,
        "node_a": node_a.reshape(n_ntiles, P).T,
        "src": src.transpose(0, 2, 1),
        "dst": dst.transpose(2, 0, 1).reshape(P, n_chunks * TILES),
        "first": dst[:, 0, 0],
        "sph": edges(a["edge_attr_4"]).transpose(0, 2, 1, 3).reshape(n_chunks, P, TILES * SPH),
    }
    for l, name in enumerate(("edge_attr_16", "edge_attr_10")):
        arrays[f"attr{l}"] = edges(a[name]).reshape(n_chunks, CHUNK, -1).transpose(0, 2, 1)
    l2s, l2v = a["L0_gnn_Wl2_s"], a["L0_gnn_Wl2_v"]
    weights = [
        {"fc1": a["L0_gnn_Wfc1"], "fc2": a["L0_gnn_Wfc2"], "t0": a["L0_gnn_Wl1_0"], "t1": a["L0_gnn_Wl1_1"],
         "s0": a["L0_gnn_Wsc0"], "s1": a["L0_gnn_Wsc1"], "a": l2s[:MUL0], "dd": l2s[MUL0:],
         "b": l2v[:MUL0], "c": l2v[MUL0:], "alpha": a["L0_gnn_Wa"]},
        {"fc1": a["L1_gnn_W_fc1"], "fc2": a["L1_gnn_W_fc2"], "t0": a["L1_gnn_W_l1_0"], "t1": a["L1_gnn_W_l1_1"],
         "s0": a["L1_gnn_W_si0"], "s1": a["L1_gnn_W_si1"], "a": a["L1_gnn_W_l2_00"], "dd": a["L1_gnn_W_l2_10"],
         "b": a["L1_gnn_W_l2_01"], "c": a["L1_gnn_W_l2_11"]},
    ]
    for l in range(2):
        arrays.update({f"L{l}_{k}": v for k, v in weights[l].items()})
    arrays = {f"in_{k}": np.ascontiguousarray(v) for k, v in arrays.items()}

    nc = bacc.Bacc("TRN2", target_bir_lowering=False, num_devices=1)
    d = {k[3:]: nc.dram_tensor(k, v.shape, mb.dt.from_np(v.dtype), kind="ExternalInput").ap()
         for k, v in arrays.items()}
    for name in ("table0", "resid0", "table1", "resid1"):
        d[name] = nc.dram_tensor(name, (n_rows, FEAT), mb.dt.float32, kind="Internal").ap()
    d["out"] = nc.dram_tensor("out_0", (n_rows, FEAT), mb.dt.float32, kind="ExternalOutput").ap()
    build(nc, d, n_nodes, n_chunks, n_ntiles)
    got = run_bass_kernel_spmd(nc, [arrays], core_ids=[0]).results[0]["out_0"][:n_nodes]
    vectors = got[:, MUL0:].reshape(-1, VEC, MUL1).transpose(0, 2, 1).reshape(-1, VEC * MUL1)
    return np.concatenate([got[:, :MUL0], vectors], axis=1)
```

```python
import math
from contextlib import ExitStack

import concourse.bass as bass
from concourse import mybir

P = 128
MUL0, MUL1, VEC = 64, 32, 3
FEAT = MUL0 + VEC * MUL1
WNUM = 2 * MUL0 + 2 * MUL1
ONE = 2 * MUL0 + VEC * MUL1 + MUL1
PROD = ONE + 1
TILES = 4
CHUNK = TILES * P
SLOTS = 4
WIN = 24
SPH = 4
HOTS = (SPH + 1) * WIN
BLOCKS = 4
BANK = 512
LN_EPS = 1e-5


def build(nc, d, n_nodes, n_chunks, n_ntiles):
    f32, i32 = mybir.dt.float32, mybir.dt.int32
    ALU, ACT = mybir.AluOpType, mybir.ActivationFunctionType
    AX = mybir.AxisListType
    n_rows = n_ntiles * P
    n_windows = -(-n_nodes // WIN)
    assert n_chunks % SLOTS == 0 and n_ntiles % 2 == 0 and n_rows >= max(n_nodes + 1 + WIN, n_windows * WIN)
    n_slots = n_chunks * CHUNK
    K1 = (16, 10)
    COLS = (2 * P, CHUNK)
    H = (64, 100)
    h_func = (ACT.Silu, ACT.Relu)
    h_scale = (1.0 / math.sqrt(K1[0]), math.sqrt(2.0) / math.sqrt(K1[1]))
    fan = math.sqrt(MUL0 + MUL1)
    conv_scale = (1.0 / math.sqrt(H[0]) / fan, 0.5 / math.sqrt(16.0) / math.sqrt(H[1]) / fan)
    ALPHA, COUNT = FEAT, FEAT + 1

    with ExitStack() as ctx:
        def sb(name, shape, dt=f32):
            return ctx.enter_context(nc.sbuf_tensor(name, shape, dt))

        def sem(name):
            return ctx.enter_context(nc.semaphore(name))

        acc = sb("acc", [P, BLOCKS, n_rows])
        first_i = sb("first_i", [P, n_chunks], i32)
        first_f = sb("first_f", [P, n_chunks])
        dst_i = sb("dst_i", [P, n_chunks * TILES], i32)
        dst_rel = sb("dst_rel", [P, n_chunks * TILES])
        dst_out = sb("dst_out", [P, n_chunks * TILES])
        inside = sb("inside", [P, n_chunks * TILES])
        n_inside = sb("n_inside", [P, 1])
        ones = sb("ones", [P, 1])
        n_outside = sb("n_outside", [1, 1], i32)
        gen_iota = sb("gen_iota", [P, WIN])
        node_a = sb("node_a", [P, n_ntiles])
        iota_i = sb("iota_i", [P, WIN], i32)
        iota = sb("iota", [P, WIN])
        row_i = sb("row_i", [P, P], i32)
        ident = sb("ident", [P, P])
        zeros = sb("zeros", [P, BLOCKS, P])
        eps = sb("eps", [P, 1])
        fc1w = [sb("fc1w0", [P, 2 * H[0]]), sb("fc1w1", [P, H[1]])]
        fc2w = [sb("fc2w0", [P, 2, WNUM]), sb("fc2w1", [H[1], 1, WNUM])]
        nodew = [sb(f"nodew{l}", [VEC * MUL1, 2, FEAT]) for l in range(2)]
        convw = [sb(f"convw{l}", [P, 2, FEAT + 2]) for l in range(2)]
        attr = sb("attr", [P, SLOTS, CHUNK])
        src = sb("src", [P, SLOTS, TILES], i32)
        sph = sb("sph", [P, SLOTS, TILES, SPH])
        rows = sb("rows", [P, SLOTS, TILES, FEAT])
        hidden = sb("hidden", [P, 2, CHUNK])
        hot = sb("hot", [P, 2, TILES, SPH + 1, WIN])
        sh_vec = sb("sh_vec", [P, 2, TILES, VEC, MUL1])
        sh_dot = sb("sh_dot", [P, 2, TILES, MUL1])
        prod = sb("prod", [P, 2, TILES, PROD])
        agg = sb("agg", [HOTS, 2, PROD + MUL1])
        x_t = sb("x_t", [VEC * MUL1, 2, 2, P])
        x_row = sb("x_row", [P, 2, FEAT])
        tab_out = sb("tab_out", [P, 2, FEAT])
        res_out = sb("res_out", [P, 2, FEAT])
        res_in = sb("res_in", [P, 2, FEAT])
        sums = sb("sums", [P, 2, BLOCKS, P])
        mixed = sb("mixed", [P, 2, FEAT])
        small = sb("small", [P, 2, 16])

        bank = [ctx.enter_context(nc.psum_tensor(f"bank{b}", [P, BANK], f32)) for b in range(8)]
        hid_ps, w_ps, agg_ps, sel_ps = bank[0:2], bank[2:6], bank[6], bank[7]
        conv_ps, trans_ps, tab_ps, self_ps = bank[0:2], bank[2:4], bank[4:6], bank[6:8]

        index_in, weights_zeroed, weights_in = sem("index_in"), sem("weights_zeroed"), sem("weights_in")
        weights_ready = sem("weights_ready")
        iota_made, consts_made, acc_zeroed = sem("iota_made"), sem("consts_made"), sem("acc_zeroed")
        attr_zeroed = sem("attr_zeroed")
        prep_step = sem("prep_step")
        attr_in = [sem(f"attr_in{k}") for k in range(SLOTS)]
        src_in = [sem(f"src_in{k}") for k in range(SLOTS)]
        sph_in = [sem(f"sph_in{k}") for k in range(SLOTS)]
        rows_in = [sem(f"rows_in{k}") for k in range(SLOTS)]
        fc1_done, hidden_ready = sem("fc1_done"), sem("hidden_ready")
        w_ready, prod_done = sem("w_ready"), sem("prod_done")
        hot_made, hot_ready = sem("hot_made"), sem("hot_ready")
        vec_made, dot_made = sem("vec_made"), sem("dot_made")
        agg_done, agg_copied = sem("agg_done"), sem("agg_copied")
        selected, acc_added = sem("selected"), sem("acc_added")
        counted, outside_ready = sem("counted"), sem("outside_ready")
        total_done = sem("total_done")
        gen_loaded, gen_rows = sem("gen_loaded"), sem("gen_rows")
        gen_fc1, gen_hidden, gen_w, gen_prod = sem("gen_fc1"), sem("gen_hidden"), sem("gen_w"), sem("gen_prod")
        gen_hot, gen_agg, gen_copied = sem("gen_hot"), sem("gen_agg"), sem("gen_copied")
        gen_selected, gen_added, gen_step = sem("gen_selected"), sem("gen_added"), sem("gen_step")
        x_in = [sem(f"x_in{j}") for j in range(2)]
        res_in_sem = [sem(f"res_in_sem{j}") for j in range(2)]
        tab_stored = [sem(f"tab_stored{j}") for j in range(2)]
        row_stored = [sem(f"row_stored{j}") for j in range(2)]
        node_mm, tab_ready, res_ready = sem("node_mm"), sem("tab_ready"), sem("res_ready")
        sums_staged, conv_done, stats_done = sem("sums_staged"), sem("conv_done"), sem("stats_done")
        std_done, rstd_made, normed = sem("std_done"), sem("rstd_made"), sem("normed")
        transposed, xt_copied, mix_step = sem("transposed"), sem("xt_copied"), sem("mix_step")
        turn = {e: sem(f"turn_{e}") for e in ("sp", "pool", "act", "dve", "pe")}

        def reached(n, least):
            return not isinstance(n, int) or n >= least

        def in_range(n, count):
            return not isinstance(n, int) or 0 <= n < count

        def chunk_no(l, c):
            return l * n_chunks + c

        def slot_loads(g, k, each=16):
            return (each // SLOTS) * (g - k) + each

        def tile_no(phase, n):
            return phase * n_ntiles + n

        def stores_before(number, j):
            return 8 * (number - j)

        def pipeline(eng, step, count, unroll, lag):
            for n in range(4):
                step(n, n % unroll)
            with eng.Fori(4 // unroll, count // unroll) as i:
                for k in range(unroll):
                    step(i * unroll + k, k)
            for n in range(count, count + lag):
                step(n, n % unroll)

        def over_chunks(eng, step, lag):
            pipeline(eng, step, n_chunks, SLOTS, lag)

        def over_tiles(eng, step, lag):
            pipeline(eng, step, n_ntiles, 2, lag)

        def in_general(eng, l, step):
            eng.wait_ge(outside_ready, 1)
            outside = eng.value_load(n_outside[0:1, 0:1], min_val=0, max_val=n_slots)
            with eng.If(outside > 0):
                with eng.Fori(0, n_chunks) as c:
                    step(c, chunk_no(l, c))

        def over_windows(eng, g, step):
            first = held(eng, g * n_windows)
            with eng.Fori(0, n_windows) as v:
                step(v, first + v)

        def held(eng, value):
            return value if isinstance(value, int) else eng.snap(value)

        def weight_loads(l):
            w = {k: d[f"L{l}_{k}"] for k in ("fc1", "fc2", "t0", "t1", "s0", "s1", "a", "b", "c", "dd")}
            out = []
            for b in range(2 - l):
                out.append((fc1w[l][K1[l] * b:K1[l] * (b + 1), H[l] * b:H[l] * (b + 1)], w["fc1"]))
                out.append((fc2w[l][H[l] * b:H[l] * (b + 1), b, :], w["fc2"]))
            for s, (w0, w1) in enumerate((("t0", "t1"), ("s0", "s1"))):
                out.append((nodew[l][0:MUL0, s, 0:MUL0], w[w0]))
                for m in range(VEC):
                    out.append((nodew[l][32 * m:32 * m + 32, s, MUL0 + 32 * m:MUL0 + 32 * m + 32], w[w1]))
            for m in range(VEC):
                out.append((convw[l][32 * m:32 * m + 32, 0, MUL0 + 32 * m:MUL0 + 32 * m + 32], w["c"]))
            out.append((convw[l][96:128, 0, 0:MUL0], w["dd"]))
            out.append((convw[l][0:MUL0, 1, 0:MUL0], w["a"]))
            out.append((convw[l][MUL0:P, 1, MUL0:MUL0 + MUL1], w["b"]))
            if l == 0:
                out.append((convw[l][96:128, 0, ALPHA:ALPHA + 1], d["L0_alpha"][MUL0:MUL0 + MUL1, :]))
                out.append((convw[l][0:MUL0, 1, ALPHA:ALPHA + 1], d["L0_alpha"][0:MUL0, :]))
            return out
        loads = weight_loads(0), weight_loads(1)
        n_weight_loads = len(loads[0]) + len(loads[1])

        block = ctx.enter_context(nc.Block())

        @block.sync
        def _(sp):
            sp.dma_start(dst_i[:, :], d["dst"]).then_inc(index_in, 16)
            sp.dma_start(first_i[:, :], d["first"].partition_broadcast(P)).then_inc(index_in, 16)
            sp.dma_start(node_a[:, :], d["node_a"]).then_inc(index_in, 16)
            sp.wait_ge(attr_zeroed, 1)
            sp.wait_ge(weights_zeroed, 8)
            for dst, source in loads[0]:
                sp.dma_start(dst, source).then_inc(weights_in, 16)

            def load_x(n, j):
                at = held(sp, n * P)
                if reached(n, 2):
                    sp.wait_ge(res_ready, n - 1)
                    sp.sem_inc(turn["sp"])
                cols = bass.ds(at, P)
                sp.dma_start(x_t[0:MUL0, j, 0, :], d["xt0"][:, cols]).then_inc(x_in[j], 16)
                sp.dma_start(x_t[:, j, 1, :], d["xt1"][:, cols]).then_inc(x_in[j], 16)
                sp.dma_start(x_row[:, j, :], d["x"][cols, :]).then_inc(x_in[j], 16)
            over_tiles(sp, load_x, 0)

            def edge_loads(l, at, k):
                one = bass.ds(at, 1)
                return ((attr[0:(2 - l) * K1[l], k, 0:COLS[l]],
                         d[f"attr{l}"][one, :, :].rearrange("o k e -> (o k) e")),
                        (src[:, k, :], d["src"][one, :, :].rearrange("o p t -> (o p) t")),
                        (sph[:, k, :, :].rearrange("p t m -> p (t m)"),
                         d["sph"][one, :, :].rearrange("o p e -> (o p) e")))

            def load_edges(l, c, k):
                g = chunk_no(l, c)
                at = held(sp, c)
                if reached(g, SLOTS):
                    sp.wait_ge(fc1_done, g - 3)
                    sp.sem_inc(turn["sp"])
                loads_of = edge_loads(l, at, k)
                sp.dma_start(*loads_of[0]).then_inc(attr_in[k], 16)
                if reached(g, SLOTS):
                    sp.wait_ge(rows_in[k], slot_loads(g - SLOTS, k, 16 * TILES))
                    sp.sem_inc(turn["sp"])
                sp.dma_start(*loads_of[1]).then_inc(src_in[k], 16)
                if reached(g, SLOTS):
                    sp.wait_ge(hot_ready, g - 3)
                    sp.sem_inc(turn["sp"])
                sp.dma_start(*loads_of[2]).then_inc(sph_in[k], 16)

            for l in range(2):
                over_chunks(sp, lambda c, k: load_edges(l, c, k), 0)
                sp.wait_ge(acc_added, chunk_no(l + 1, 0))

                def general(c, g):
                    at = held(sp, c)
                    sp.wait_ge(gen_added, g * n_windows + 1)
                    sp.sem_inc(turn["sp"])
                    for dst, source in edge_loads(l, at, 0):
                        sp.dma_start(dst, source).then_inc(gen_loaded, 16)
                in_general(sp, l, general)
                phase = l + 1
                for j in range(2):
                    sp.wait_ge(row_stored[j], stores_before(tile_no(phase, j), j))

                def load_res(n, j):
                    at = held(sp, n * P)
                    if reached(tile_no(l, n), 2):
                        sp.wait_ge(stats_done, tile_no(l, n) - 1)
                        sp.sem_inc(turn["sp"])
                    sp.dma_start(res_in[:, j, :], d[f"resid{l}"][bass.ds(at, P), :]).then_inc(res_in_sem[j], 16)
                over_tiles(sp, load_res, 0)

        @block.gpsimd
        def _(pool):
            nc.gpsimd.iota(iota_i[:, :], pattern=[[1, WIN]], base=0, channel_multiplier=0).then_inc(iota_made, 1)
            nc.gpsimd.iota(row_i[:, :], pattern=[[1, P]], base=0, channel_multiplier=-1).then_inc(iota_made, 1)
            nc.gpsimd.memset(zeros[:, :, :], 0.0).then_inc(consts_made, 1)
            nc.gpsimd.memset(acc[:, :, :], 0.0).then_inc(acc_zeroed, 1)

            def store_rows(phase, n, j):
                at = held(pool, n * P)
                rows_at = bass.ds(at, P)
                pool.wait_ge(tab_ready, tile_no(phase, n) + 1)
                pool.sem_inc(turn["pool"])
                pool.dma_start(d[f"table{phase}"][rows_at, :], tab_out[:, j, :]).then_inc(tab_stored[j], 16)
                pool.wait_ge(res_ready, tile_no(phase, n) + 1)
                pool.sem_inc(turn["pool"])
                pool.dma_start(d[f"resid{phase}"][rows_at, :], res_out[:, j, :]).then_inc(row_stored[j], 16)
            over_tiles(pool, lambda n, j: store_rows(0, n, j), 0)

            def gather_tile(l, k, t):
                return nc.gpsimd.indirect_dma_start(
                    out=rows[:, k, t, :], out_offset=None, in_=d[f"table{l}"],
                    in_offset=bass.IndirectOffsetOnAxis(ap=src[:, k, t:t + 1], axis=0))

            def gather(l, c, k):
                g = chunk_no(l, c)
                if reached(g, SLOTS):
                    pool.wait_ge(prod_done, 2 * (g - 3))
                pool.wait_ge(src_in[k], slot_loads(g, k))
                pool.sem_inc(turn["pool"])
                for t in range(TILES):
                    gather_tile(l, k, t).then_inc(rows_in[k], 16)

            for l in range(2):
                for j in range(2):
                    pool.wait_ge(tab_stored[j], stores_before(tile_no(l + 1, j), j))
                over_chunks(pool, lambda c, k: gather(l, c, k), 0)

                def general(c, g):
                    pool.wait_ge(gen_loaded, 48 * (g + 1))
                    pool.sem_inc(turn["pool"])
                    for t in range(TILES):
                        gather_tile(l, 0, t).then_inc(gen_rows, 16)
                in_general(pool, l, general)
                if l == 0:
                    pool.wait_ge(consts_made, 2)

                    def between(n, j):
                        if in_range(n - 3, n_ntiles):
                            store_rows(1, n - 3, 1 - j)
                        if in_range(n, n_ntiles):
                            at = held(pool, n * P)
                            pool.wait_ge(sums_staged, n + 1)
                            pool.sem_inc(turn["pool"])
                            nc.gpsimd.tensor_copy(acc[:, :, bass.ds(at, P)], zeros[:, :, :]).then_inc(acc_zeroed, 1)
                    over_tiles(pool, between, 3)

            def store_out(n, j):
                at = held(pool, n * P)
                pool.wait_ge(normed, tile_no(1, n) + 1)
                pool.sem_inc(turn["pool"])
                pool.dma_start(d["out"][bass.ds(at, P), :], x_row[:, j, :]).then_inc(row_stored[j], 16)
            over_tiles(pool, store_out, 0)
            for j in range(2):
                pool.wait_ge(row_stored[j], stores_before(tile_no(3, j), j))
                pool.wait_ge(tab_stored[j], stores_before(tile_no(2, j), j))

        @block.scalar
        def _(act):
            act.wait_ge(weights_zeroed, 8)
            for dst, source in loads[1]:
                act.dma_start(dst, source).then_inc(weights_in, 16)
            act.wait_ge(index_in, 48)

            def table_out(phase, n, j):
                number, at = tile_no(phase, n), held(act, n)
                act.wait_ge(node_mm, number + 1)
                if reached(number, 2):
                    act.wait_ge(tab_stored[j], stores_before(number, j))
                    act.sem_inc(turn["act"])
                nc.scalar.activation(tab_out[:, j, :], tab_ps[j][:, 0:FEAT], ACT.Copy,
                                     scale=node_a[:, bass.ds(at, 1)]).then_inc(tab_ready, 1)
            over_tiles(act, lambda n, j: table_out(0, n, j), 0)

            def hidden_act(l, c, k):
                g = chunk_no(l, c)
                act.wait_ge(fc1_done, g + 1)
                if reached(g, 2):
                    act.wait_ge(w_ready, 2 * (g - 1))
                activate(l, k).then_inc(hidden_ready, 1)

            def activate(l, k):
                n = H[l] * (2 - l)
                return nc.scalar.activation(hidden[0:n, k % 2, 0:COLS[l]], hid_ps[k % 2][0:n, 0:COLS[l]], h_func[l],
                                            scale=h_scale[l])

            def copy_agg(k):
                d_at = 2 * MUL0 + VEC * MUL1
                nc.scalar.activation(agg[:, k % 2, 0:d_at], agg_ps[0:HOTS, 0:d_at], ACT.Copy)
                return nc.scalar.activation(agg[:, k % 2, d_at + MUL1:], agg_ps[0:HOTS, d_at:PROD], ACT.Copy)

            def copy_sums(l, c, k):
                g = chunk_no(l, c)
                act.wait_ge(agg_done, g + 1)
                if reached(g, 2):
                    act.wait_ge(selected, g - 1)
                copy_agg(k).then_inc(agg_copied, 1)

            def node_step(l, n, j):
                if in_range(n, n_ntiles):
                    at, number = held(act, n * P), tile_no(l, n)
                    if reached(number, 2):
                        act.wait_ge(conv_done, number - 1)
                        act.sem_inc(turn["act"])
                    nc.scalar.copy(sums[:, j, :, :], acc[:, :, bass.ds(at, P)]).then_inc(sums_staged, 1)
                if in_range(n - 1, n_ntiles):
                    act.wait_ge(stats_done, tile_no(l, n - 1) + 1)
                    nc.scalar.activation(small[:, 1 - j, 12:13], small[:, 1 - j, 11:12], ACT.Sqrt,
                                         bias=eps[:, 0:1]).then_inc(std_done, 1)
                if l == 0 and in_range(n - 2, n_ntiles):
                    act.wait_ge(transposed, n - 1)
                    if reached(n - 2, 2):
                        act.wait_ge(node_mm, tile_no(1, n - 4) + 1)
                        act.sem_inc(turn["act"])
                    nc.scalar.copy(x_t[0:MUL0, j, 0, :], trans_ps[j][0:MUL0, 0:P])
                    nc.scalar.copy(x_t[:, j, 1, :], trans_ps[j][0:VEC * MUL1, P:2 * P]).then_inc(xt_copied, 1)
                if l == 0 and in_range(n - 3, n_ntiles):
                    table_out(1, n - 3, 1 - j)

            act.wait_ge(consts_made, 2)
            for l in range(2):
                def chunk_step(c, k):
                    if in_range(c, n_chunks):
                        hidden_act(l, c, k)
                    if in_range(c - 2, n_chunks):
                        copy_sums(l, c - 2, (k - 2) % SLOTS)
                over_chunks(act, chunk_step, 2)
                act.wait_ge(acc_added, chunk_no(l + 1, 0))

                def general(c, g):
                    act.wait_ge(gen_fc1, g + 1)
                    activate(l, 0).then_inc(gen_hidden, 1)

                    def window(v, number):
                        act.wait_ge(gen_agg, number + 1)
                        copy_agg(0).then_inc(gen_copied, 1)
                        act.wait_ge(gen_added, number + 2)
                    over_windows(act, g, window)
                in_general(act, l, general)
                over_tiles(act, lambda n, j: node_step(l, n, j), 3 if l == 0 else 1)

        @block.vector
        def _(dve):
            steps = [0]

            def own(ins):
                steps[0] += 1
                ins.then_inc(prep_step, 1)
                dve.wait_ge(prep_step, steps[0])

            for l in range(2):
                nc.vector.memset(nodew[l][:, :, :], 0.0).then_inc(weights_zeroed, 1)
                nc.vector.memset(convw[l][:, :, :], 0.0).then_inc(weights_zeroed, 1)
                nc.vector.memset(fc1w[l][:, :], 0.0).then_inc(weights_zeroed, 1)
                nc.vector.memset(fc2w[l][:, :, :], 0.0).then_inc(weights_zeroed, 1)
            nc.vector.memset(attr[:, :, :], 0.0).then_inc(attr_zeroed, 1)
            nc.vector.memset(agg[:, :, :], 0.0)
            for k in range(2):
                nc.vector.memset(prod[:, k, :, ONE:PROD], 1.0)
            nc.vector.memset(eps[:, :], LN_EPS).then_inc(consts_made, 1)
            nc.vector.memset(ones[:, :], 1.0)
            dve.sem_inc(gen_added)
            dve.wait_ge(iota_made, 2)
            nc.vector.tensor_copy(iota[:, :], iota_i[:, :])
            own(nc.vector.tensor_scalar(ident[:, :], row_i[:, :], 0.0, None, ALU.is_equal))
            dve.wait_ge(index_in, 48)
            nc.vector.tensor_copy(dst_out[:, :], dst_i[:, :])
            own(nc.vector.tensor_copy(first_f[:, :], first_i[:, :]))
            own(nc.vector.tensor_tensor(
                dst_rel[:, :].rearrange("p (c t) -> p c t", t=TILES),
                dst_out[:, :].rearrange("p (c t) -> p c t", t=TILES),
                first_f[:, :].unsqueeze(2).broadcast_to([P, n_chunks, TILES]), ALU.subtract))
            own(nc.vector.tensor_scalar(inside[:, :], dst_rel[:, :], float(WIN), None, ALU.is_lt))
            own(nc.vector.scalar_tensor_tensor(out=inside[:, :], in0=dst_rel[:, :], scalar=0.0, in1=inside[:, :],
                                               op0=ALU.is_ge, op1=ALU.mult))
            nc.vector.tensor_reduce(n_inside[:, :], inside[:, :], AX.X, ALU.add).then_inc(counted, 1)
            own(nc.vector.scalar_tensor_tensor(out=dst_out[:, :], in0=inside[:, :], scalar=-float(2 * n_rows),
                                               in1=dst_out[:, :], op0=ALU.mult, op1=ALU.add))
            dve.wait_ge(total_done, 1)
            nc.vector.tensor_scalar(n_outside[:, :], bank[7][0:1, 0:1], -1.0, float(n_slots),
                                    ALU.mult, ALU.add).then_inc(outside_ready, 1)
            dve.wait_ge(weights_in, 16 * n_weight_loads)
            for l in range(2):
                nc.vector.tensor_scalar(nodew[l][:, :, 0:MUL0], nodew[l][:, :, 0:MUL0],
                                        1.0 / math.sqrt(MUL0), None, ALU.mult)
                nc.vector.tensor_scalar(nodew[l][:, :, MUL0:FEAT], nodew[l][:, :, MUL0:FEAT],
                                        1.0 / math.sqrt(MUL1), None, ALU.mult)
                own(nc.vector.tensor_scalar(convw[l][:, :, :], convw[l][:, :, :], conv_scale[l], None, ALU.mult))
                third = 1.0 / math.sqrt(VEC)
                own(nc.vector.tensor_scalar(convw[l][96:128, 0, 0:MUL0], convw[l][96:128, 0, 0:MUL0],
                                            third, None, ALU.mult))
            own(nc.vector.tensor_scalar(convw[0][96:128, 0, ALPHA:ALPHA + 1], convw[0][96:128, 0, ALPHA:ALPHA + 1],
                                        third, None, ALU.mult))
            nc.vector.tensor_copy(small[:, 0, 0:1], eps[:, :]).then_inc(weights_ready, 1)

            def resid_out(phase, n, j):
                number, at = tile_no(phase, n), held(dve, n)
                dve.wait_ge(node_mm, number + 1)
                if reached(number, 2):
                    dve.wait_ge(row_stored[j], stores_before(number, j))
                    dve.sem_inc(turn["dve"])
                nc.vector.scalar_tensor_tensor(out=res_out[:, j, :], in0=self_ps[j][:, 0:FEAT],
                                               scalar=node_a[:, bass.ds(at, 1)], in1=x_row[:, j, :],
                                               op0=ALU.mult, op1=ALU.add).then_inc(res_ready, 1)

            def pre_step(n, j):
                dve.wait_ge(x_in[j], stores_before(n, j) * 3 + 48)
                resid_out(0, n, j)
            over_tiles(dve, pre_step, 0)

            def spread_hot(k):
                return nc.vector.tensor_tensor(
                    hot[:, k % 2, :, 0:SPH, :],
                    hot[:, k % 2, :, SPH:SPH + 1, :].broadcast_to([P, TILES, SPH, WIN]),
                    sph[:, k, :, :].unsqueeze(3).broadcast_to([P, TILES, SPH, WIN]), ALU.mult)

            def sh_times(k):
                return nc.vector.tensor_tensor(
                    sh_vec[:, k % 2, :, :, :], rows[:, k, :, MUL0:FEAT].rearrange("p t (m u) -> p t m u", m=VEC),
                    sph[:, k, :, 1:SPH].unsqueeze(3).broadcast_to([P, TILES, VEC, MUL1]), ALU.mult)

            def sh_sum(k):
                return nc.vector.tensor_reduce(sh_dot[:, k % 2, :, :],
                                               sh_vec[:, k % 2, :, :, :].rearrange("p t m u -> p t u m"),
                                               AX.X, ALU.add)

            def windows(l, c, k):
                g, at = chunk_no(l, c), held(dve, c * TILES)
                if reached(g, 2):
                    dve.wait_ge(agg_done, g - 1)
                    dve.sem_inc(turn["dve"])
                nc.vector.tensor_tensor(
                    hot[:, k % 2, :, SPH, :], iota[:, :].unsqueeze(1).broadcast_to([P, TILES, WIN]),
                    dst_rel[:, bass.ds(at, TILES)].unsqueeze(2).broadcast_to([P, TILES, WIN]),
                    ALU.is_equal).then_inc(hot_made, 1)
                dve.wait_ge(rows_in[k], slot_loads(g, k, 16 * TILES))
                dve.wait_ge(sph_in[k], slot_loads(g, k))
                sh_times(k).then_inc(vec_made, 1)
                dve.wait_ge(hot_made, g + 1)
                spread_hot(k).then_inc(hot_ready, 1)
                dve.wait_ge(vec_made, g + 1)
                sh_sum(k).then_inc(dot_made, 1)

            def multiply(k, q):
                w = w_ps[2 * (k % 2) + q][:, 0:2 * WNUM].rearrange("p (t n) -> p t n", t=2)
                out = prod[:, k % 2, 2 * q:2 * q + 2, :]
                row = rows[:, k, 2 * q:2 * q + 2, :]
                nc.vector.tensor_tensor(
                    out[:, :, 0:2 * MUL0].rearrange("p t (s u) -> p t s u", s=2),
                    w[:, :, 0:2 * MUL0].rearrange("p t (s u) -> p t s u", s=2),
                    row[:, :, 0:MUL0].unsqueeze(2).broadcast_to([P, 2, 2, MUL0]), ALU.mult)
                at, d_at = 2 * MUL0, 2 * MUL0 + VEC * MUL1
                nc.vector.tensor_tensor(
                    out[:, :, at:d_at].rearrange("p t (m u) -> p t m u", m=VEC),
                    w[:, :, at:at + MUL1].unsqueeze(2).broadcast_to([P, 2, VEC, MUL1]),
                    row[:, :, MUL0:FEAT].rearrange("p t (m u) -> p t m u", m=VEC), ALU.mult)
                return nc.vector.tensor_tensor(out[:, :, d_at:d_at + MUL1], w[:, :, at + MUL1:WNUM],
                                               sh_dot[:, k % 2, 2 * q:2 * q + 2, :], ALU.mult)

            def products(l, c, k):
                g = chunk_no(l, c)
                dve.wait_ge(dot_made, g + 1)
                for q in range(2):
                    dve.wait_ge(w_ready, 2 * g + q + 1)
                    multiply(k, q).then_inc(prod_done, 1)

            def add_window(l, nodes):
                ps = sel_ps
                nc.vector.tensor_tensor(acc[0:MUL0, 0, nodes], acc[0:MUL0, 0, nodes], ps[0:MUL0, 0:WIN], ALU.add)
                nc.vector.tensor_tensor(acc[MUL0:P, 0:VEC, nodes], acc[MUL0:P, 0:VEC, nodes],
                                        ps[MUL0:P, WIN:SPH * WIN].rearrange("p (m w) -> p m w", m=VEC), ALU.add)
                if l == 0:
                    nc.vector.tensor_tensor(acc[0:1, 1, nodes], acc[0:1, 1, nodes],
                                            ps[0:1, HOTS:HOTS + WIN], ALU.add)
                return nc.vector.tensor_tensor(acc[:, VEC, nodes], acc[:, VEC, nodes],
                                               ps[:, SPH * WIN:HOTS], ALU.add)

            def add_sums(l, c, k):
                g = chunk_no(l, c)
                at = dve.value_load(first_i[0:1, bass.ds(c, 1)], min_val=0, max_val=n_nodes)
                dve.wait_ge(selected, g + 1)
                if reached(g, 1):
                    dve.wait_ge(acc_added, g)
                    dve.sem_inc(turn["dve"])
                add_window(l, bass.ds(at, WIN)).then_inc(acc_added, 1)

            def mix(l, n, j):
                number, at = tile_no(l, n), held(dve, n)
                done = 6 * number if l == 0 else 6 * n_ntiles + 3 * n
                ps, res = conv_ps[j], res_in[:, j, :]
                dve.wait_ge(res_in_sem[j], stores_before(number, j) + 16)
                dve.wait_ge(conv_done, number + 1)
                s = [small[:, j, i:i + 1] for i in range(16)]
                a = node_a[:, bass.ds(at, 1)]
                count = [0]

                def after(ins):
                    count[0] += 1
                    ins.then_inc(mix_step, 1)
                    dve.wait_ge(mix_step, done + count[0])
                    dve.sem_inc(turn["dve"])
                if l == 0:
                    dve.sem_inc(turn["dve"])
                    after(nc.vector.tensor_scalar(s[0], ps[:, COUNT:COUNT + 1], 1.0, None, ALU.max))
                    after(nc.vector.reciprocal(s[1], s[0]))
                    after(nc.vector.tensor_tensor(s[2], s[1], a, ALU.mult))
                    after(nc.vector.tensor_scalar(s[3], ps[:, ALPHA:ALPHA + 1], s[2], s[2], ALU.mult, ALU.mult))
                else:
                    dve.sem_inc(turn["dve"])
                    after(nc.vector.tensor_copy(s[3], a))
                after(nc.vector.scalar_tensor_tensor(out=mixed[:, j, :], in0=ps[:, 0:FEAT], scalar=s[3], in1=res,
                                                     op0=ALU.mult, op1=ALU.add))
                after(nc.vector.bn_stats(s_stats(j), mixed[:, j, :]))
                nc.vector.bn_aggr(small[:, j, 10:12], s_stats(j)).then_inc(stats_done, 1)

            def s_stats(j):
                return small[:, j, 4:10]

            def norm(l, n, j):
                number = tile_no(l, n)
                dve.wait_ge(std_done, number + 1)
                nc.vector.reciprocal(small[:, j, 13:14], small[:, j, 12:13]).then_inc(rstd_made, 1)
                if l == 0 and reached(n, 2):
                    dve.wait_ge(transposed, n - 1)
                if l == 1:
                    dve.wait_ge(row_stored[j], stores_before(tile_no(2, n), j))
                dve.wait_ge(rstd_made, number + 1)
                dve.sem_inc(turn["dve"])
                nc.vector.tensor_scalar(x_row[:, j, :], mixed[:, j, :], small[:, j, 10:11], small[:, j, 13:14],
                                        ALU.subtract, ALU.mult).then_inc(normed, 1)

            def node_step(l, n, j):
                if l == 0 and in_range(n - 3, n_ntiles):
                    resid_out(1, n - 3, 1 - j)
                if in_range(n, n_ntiles):
                    mix(l, n, j)
                if in_range(n - 1, n_ntiles):
                    norm(l, n - 1, 1 - j)

            dve.wait_ge(acc_zeroed, 1)
            for l in range(2):
                def chunk_step(c, k):
                    if in_range(c, n_chunks):
                        windows(l, c, k)
                    if in_range(c - 3, n_chunks):
                        add_sums(l, c - 3, (k - 3) % SLOTS)
                    if in_range(c, n_chunks):
                        products(l, c, k)
                over_chunks(dve, chunk_step, 3)

                def general(c, g):
                    tiles = bass.ds(held(dve, c * TILES), TILES)
                    steps_before = held(dve, g * (3 + 2 * n_windows))
                    dve.wait_ge(gen_loaded, 48 * (g + 1))
                    dve.wait_ge(gen_rows, 16 * TILES * (g + 1))
                    sh_times(0).then_inc(gen_step, 1)
                    dve.wait_ge(gen_step, steps_before + 1)
                    sh_sum(0).then_inc(gen_step, 1)
                    nc.vector.tensor_copy(gen_iota[:, :], iota[:, :]).then_inc(gen_step, 1)
                    dve.wait_ge(gen_w, g + 1)
                    dve.wait_ge(gen_step, steps_before + 3)
                    multiply(0, 0)
                    multiply(0, 1).then_inc(gen_prod, 1)

                    def window(v, number):
                        nodes = bass.ds(held(dve, v * WIN), WIN)
                        before = held(dve, steps_before + (v * 2 + 3))
                        nc.vector.tensor_tensor(
                            hot[:, 0, :, SPH, :], gen_iota[:, :].unsqueeze(1).broadcast_to([P, TILES, WIN]),
                            dst_out[:, tiles].unsqueeze(2).broadcast_to([P, TILES, WIN]),
                            ALU.is_equal).then_inc(gen_step, 1)
                        dve.wait_ge(gen_step, before + 1)
                        nc.vector.tensor_scalar(gen_iota[:, :], gen_iota[:, :], float(WIN), None,
                                                ALU.add).then_inc(gen_step, 1)
                        spread_hot(0).then_inc(gen_hot, 1)
                        dve.wait_ge(gen_step, before + 2)
                        dve.wait_ge(gen_selected, number + 1)
                        add_window(l, nodes).then_inc(gen_added, 1)
                        dve.wait_ge(gen_added, number + 2)
                        dve.sem_inc(turn["dve"])
                    over_windows(dve, g, window)
                in_general(dve, l, general)
                over_tiles(dve, lambda n, j: node_step(l, n, j), 3 if l == 0 else 1)
                if l == 0:
                    dve.wait_ge(acc_zeroed, 1 + n_ntiles)

        @block.tensor
        def _(pe):
            mm = nc.tensor.matmul
            pe.wait_ge(counted, 1)
            mm(bank[7][0:1, 0:1], n_inside[:, :], ones[:, :], start=True, stop=True).then_inc(total_done, 1)
            pe.wait_ge(weights_ready, 1)

            def node_maps(phase, n, j):
                number, w = tile_no(phase, n), nodew[phase]
                if reached(number, 2):
                    pe.wait_ge(tab_ready, number - 1)
                    pe.wait_ge(res_ready, number - 1)
                if phase == 0:
                    pe.wait_ge(x_in[j], stores_before(n, j) * 3 + 48)
                else:
                    pe.wait_ge(xt_copied, n + 1)
                for s, ps in enumerate((tab_ps[j], self_ps[j])):
                    mm(ps[:, 0:MUL0], x_t[0:MUL0, j, 0, :], w[0:MUL0, s, 0:MUL0], start=True, stop=True)
                    last = mm(ps[:, MUL0:FEAT], x_t[:, j, 1, :], w[:, s, MUL0:FEAT], start=True, stop=True)
                last.then_inc(node_mm, 1)
            over_tiles(pe, lambda n, j: node_maps(0, n, j), 0)

            def fc1_mm(l, k):
                n = H[l] * (2 - l)
                return mm(hid_ps[k % 2][0:n, 0:COLS[l]], fc1w[l][:, :], attr[:, k, 0:COLS[l]], start=True, stop=True)

            def fc1(l, c, k):
                g = chunk_no(l, c)
                if reached(g, 2):
                    pe.wait_ge(hidden_ready, g - 1)
                pe.wait_ge(attr_in[k], slot_loads(g, k))
                fc1_mm(l, k).then_inc(fc1_done, 1)

            def fc2_mm(l, k, q):
                ps = w_ps[2 * (k % 2) + q]
                if l == 0:
                    return mm(ps[:, 0:2 * WNUM], hidden[:, k % 2, q * P:(q + 1) * P],
                              fc2w[0][:, :, :].rearrange("p b n -> p (b n)"), start=True, stop=True)
                for t in range(2):
                    e = (2 * q + t) * P
                    last = mm(ps[:, t * WNUM:(t + 1) * WNUM], hidden[0:H[1], k % 2, e:e + P], fc2w[1][:, 0, :],
                              start=True, stop=True)
                return last

            def fc2(l, c, k):
                g = chunk_no(l, c)
                pe.wait_ge(hidden_ready, g + 1)
                for q in range(2):
                    if reached(g, 2):
                        pe.wait_ge(prod_done, 2 * (g - 2) + q + 1)
                    fc2_mm(l, k, q).then_inc(w_ready, 1)

            def agg_mm(k):
                for t in range(TILES):
                    last = mm(agg_ps[0:HOTS, 0:PROD], hot[:, k % 2, t, :, :].rearrange("p b w -> p (b w)"),
                              prod[:, k % 2, t, :], start=(t == 0), stop=(t == TILES - 1))
                return last

            def sum_edges(l, c, k):
                g = chunk_no(l, c)
                if reached(g, 1):
                    pe.wait_ge(agg_copied, g)
                pe.wait_ge(hot_ready, g + 1)
                pe.wait_ge(prod_done, 2 * g + 2)
                agg_mm(k).then_inc(agg_done, 1)

            def select_mm(l, k):
                s, c_at = agg[:, k % 2, :], 2 * MUL0
                mm(sel_ps[:, 0:SPH * WIN], s[:, 0:c_at], ident[0:HOTS, 0:SPH * WIN],
                   start=True, stop=False, skip_group_check=True)
                mm(sel_ps[:, SPH * WIN:HOTS], s[:, c_at:c_at + P], ident[0:HOTS, 0:WIN],
                   start=False, stop=False, skip_group_check=True)
                last = mm(sel_ps[96:P, SPH * WIN:HOTS], s[:, c_at + P:c_at + P + MUL1],
                          ident[0:HOTS, SPH * WIN:HOTS], start=False, stop=True, skip_group_check=True)
                if l == 0:
                    last = mm(sel_ps[0:1, HOTS:HOTS + WIN], s[:, c_at + P + MUL1:c_at + P + MUL1 + 1],
                              ident[0:HOTS, SPH * WIN:HOTS], start=False, stop=True, skip_group_check=True)
                return last

            def select(l, c, k):
                g = chunk_no(l, c)
                pe.wait_ge(agg_copied, g + 1)
                if reached(g, 1):
                    pe.wait_ge(acc_added, g)
                select_mm(l, k).then_inc(selected, 1)

            def conv(l, n, j):
                number, ps, w, cols = tile_no(l, n), conv_ps[j], convw[l], FEAT + 1 - l
                if reached(number, 2):
                    pe.wait_ge(stats_done, number - 1)
                pe.wait_ge(sums_staged, number + 1)
                mm(ps[:, 0:cols], sums[:, j, 3, :], w[:, 0, 0:cols], start=True, stop=False, skip_group_check=True)
                last = mm(ps[:, 0:cols], sums[:, j, 0, :], w[:, 1, 0:cols], start=False, stop=True,
                          skip_group_check=True)
                if l == 0:
                    last = mm(ps[:, COUNT:COUNT + 1], sums[0:MUL1, j, 1, :], ident[0:MUL1, 0:1],
                              start=False, stop=True, skip_group_check=True)
                for m in (1, 2):
                    at = MUL0 + m * MUL1
                    last = mm(ps[:, at:at + MUL1], sums[MUL0:P, j, m, :], w[MUL0:P, 1, MUL0:MUL0 + MUL1],
                              start=False, stop=True, skip_group_check=True)
                last.then_inc(conv_done, 1)

            def transpose(n, j):
                if reached(n, 2):
                    pe.wait_ge(xt_copied, n - 1)
                pe.wait_ge(normed, n + 1)
                pe.sem_inc(turn["pe"])
                nc.tensor.transpose(trans_ps[j][0:MUL0, 0:P], x_row[:, j, 0:MUL0], ident[:, :])
                nc.tensor.transpose(trans_ps[j][0:VEC * MUL1, P:2 * P], x_row[:, j, MUL0:FEAT],
                                    ident[:, :]).then_inc(transposed, 1)

            def node_step(l, n, j):
                if l == 0 and in_range(n - 3, n_ntiles):
                    node_maps(1, n - 3, 1 - j)
                if in_range(n, n_ntiles):
                    conv(l, n, j)
                if l == 0 and in_range(n - 2, n_ntiles):
                    transpose(n - 2, j)

            for l in range(2):
                def chunk_step(c, k):
                    if in_range(c, n_chunks):
                        fc1(l, c, k)
                    if in_range(c - 1, n_chunks):
                        fc2(l, c - 1, (k - 1) % SLOTS)
                    if in_range(c - 2, n_chunks):
                        sum_edges(l, c - 2, (k - 2) % SLOTS)
                    if in_range(c - 3, n_chunks):
                        select(l, c - 3, (k - 3) % SLOTS)
                over_chunks(pe, chunk_step, 3)

                def general(c, g):
                    pe.wait_ge(gen_loaded, 48 * (g + 1))
                    fc1_mm(l, 0).then_inc(gen_fc1, 1)
                    pe.wait_ge(gen_hidden, g + 1)
                    fc2_mm(l, 0, 0)
                    fc2_mm(l, 0, 1).then_inc(gen_w, 1)
                    pe.wait_ge(gen_prod, g + 1)
                    pe.sem_inc(turn["pe"])

                    def window(v, number):
                        pe.wait_ge(gen_hot, number + 1)
                        agg_mm(0).then_inc(gen_agg, 1)
                        pe.wait_ge(gen_copied, number + 1)
                        pe.wait_ge(gen_added, number + 1)
                        select_mm(l, 0).then_inc(gen_selected, 1)
                    over_windows(pe, g, window)
                in_general(pe, l, general)
                over_tiles(pe, lambda n, j: node_step(l, n, j), 3 if l == 0 else 0)


def kernel(**inputs):
    import numpy as np
    import concourse.bacc as bacc
    from concourse import mybir as mb
    from concourse.bass_utils import run_bass_kernel_spmd

    a = {k: np.asarray(v) for k, v in inputs.items()}
    n_nodes, n_edges = a["x"].shape[0], a["src"].shape[0]
    n_chunks = -(-n_edges // (CHUNK * SLOTS)) * SLOTS
    n_ntiles = -(-(n_nodes + 1 + WIN) // (2 * P)) * 2
    n_rows, pad = n_ntiles * P, n_chunks * CHUNK - n_edges

    def component_major(x):
        return x.reshape(-1, MUL1, VEC).transpose(0, 2, 1).reshape(-1, VEC * MUL1)

    x = np.zeros((n_rows, FEAT), a["x"].dtype)
    x[:n_nodes, :MUL0] = a["x"][:, :MUL0]
    x[:n_nodes, MUL0:] = component_major(a["x"][:, MUL0:])
    node_a = np.zeros((n_rows, 1), a["node_vec1"].dtype)
    node_a[:n_nodes] = a["node_vec1"]
    src = np.concatenate([a["src"], np.zeros(pad, a["src"].dtype)]).reshape(n_chunks, TILES, P)
    dst = np.concatenate([a["dst"], np.full(pad, n_nodes, a["dst"].dtype)]).reshape(n_chunks, TILES, P)

    def edges(v):
        return np.concatenate([v, np.zeros((pad, v.shape[1]), v.dtype)]).reshape(n_chunks, TILES, P, v.shape[1])
    arrays = {
        "x": x, "xt0": x[:, :MUL0].T, "xt1": x[:, MUL0:].T,
        "node_a": node_a.reshape(n_ntiles, P).T,
        "src": src.transpose(0, 2, 1),
        "dst": dst.transpose(2, 0, 1).reshape(P, n_chunks * TILES),
        "first": dst[:, 0, 0],
        "sph": edges(a["edge_attr_4"]).transpose(0, 2, 1, 3).reshape(n_chunks, P, TILES * SPH),
    }
    attr = edges(a["edge_attr_16"])
    arrays["attr0"] = attr.reshape(n_chunks, 2, 2, P, -1).transpose(0, 2, 4, 1, 3).reshape(n_chunks, -1, 2 * P)
    arrays["attr1"] = edges(a["edge_attr_10"]).reshape(n_chunks, CHUNK, -1).transpose(0, 2, 1)
    l2s, l2v = a["L0_gnn_Wl2_s"], a["L0_gnn_Wl2_v"]
    weights = [
        {"fc1": a["L0_gnn_Wfc1"], "fc2": a["L0_gnn_Wfc2"], "t0": a["L0_gnn_Wl1_0"], "t1": a["L0_gnn_Wl1_1"],
         "s0": a["L0_gnn_Wsc0"], "s1": a["L0_gnn_Wsc1"], "a": l2s[:MUL0], "dd": l2s[MUL0:],
         "b": l2v[:MUL0], "c": l2v[MUL0:], "alpha": a["L0_gnn_Wa"]},
        {"fc1": a["L1_gnn_W_fc1"], "fc2": a["L1_gnn_W_fc2"], "t0": a["L1_gnn_W_l1_0"], "t1": a["L1_gnn_W_l1_1"],
         "s0": a["L1_gnn_W_si0"], "s1": a["L1_gnn_W_si1"], "a": a["L1_gnn_W_l2_00"], "dd": a["L1_gnn_W_l2_10"],
         "b": a["L1_gnn_W_l2_01"], "c": a["L1_gnn_W_l2_11"]},
    ]
    for l in range(2):
        arrays.update({f"L{l}_{k}": v for k, v in weights[l].items()})
    arrays = {f"in_{k}": np.ascontiguousarray(v) for k, v in arrays.items()}

    nc = bacc.Bacc("TRN2", target_bir_lowering=False, num_devices=1)
    d = {k[3:]: nc.dram_tensor(k, v.shape, mb.dt.from_np(v.dtype), kind="ExternalInput").ap()
         for k, v in arrays.items()}
    for name in ("table0", "resid0", "table1", "resid1"):
        d[name] = nc.dram_tensor(name, (n_rows, FEAT), mb.dt.float32, kind="Internal").ap()
    d["out"] = nc.dram_tensor("out_0", (n_rows, FEAT), mb.dt.float32, kind="ExternalOutput").ap()
    build(nc, d, n_nodes, n_chunks, n_ntiles)
    got = run_bass_kernel_spmd(nc, [arrays], core_ids=[0]).results[0]["out_0"][:n_nodes]
    vectors = got[:, MUL0:].reshape(-1, VEC, MUL1).transpose(0, 2, 1).reshape(-1, VEC * MUL1)
    return np.concatenate([got[:, :MUL0], vectors], axis=1)
```

```python
import math
from contextlib import ExitStack

import concourse.bass as bass
from concourse import mybir

P = 128
MUL0, MUL1, VEC = 64, 32, 3
FEAT = MUL0 + VEC * MUL1
WNUM = 2 * MUL0 + 2 * MUL1
C_AT, D_AT = 2 * MUL0, 2 * MUL0 + VEC * MUL1
PROD = D_AT + MUL1
TILES = 4
CHUNK = TILES * P
SLOTS = 4
WIN = 24
SPH = 4
CD_COLS = SPH * WIN
COUNT_COLS = CD_COLS + WIN
BLOCKS = 4
BANK = 512
QUAD = 4 * P
LN_EPS = 1e-5


def build(nc, d, n_nodes, n_chunks, n_ntiles):
    f32, i32 = mybir.dt.float32, mybir.dt.int32
    ALU, ACT = mybir.AluOpType, mybir.ActivationFunctionType
    AX = mybir.AxisListType
    n_rows = n_ntiles * P
    n_windows = -(-n_nodes // WIN)
    assert n_chunks % SLOTS == 0 and n_ntiles % 4 == 0 and n_rows >= max(n_nodes + 1 + WIN, n_windows * WIN)
    assert n_chunks <= 2 * PROD, "inside stands in prod's place"
    n_slots = n_chunks * CHUNK
    K1 = (16, 10)
    COLS = (2 * P, CHUNK)
    H = (64, 100)
    h_func = (ACT.Silu, ACT.Relu)
    h_scale = (1.0 / math.sqrt(K1[0]), math.sqrt(2.0) / math.sqrt(K1[1]))
    fan = math.sqrt(MUL0 + MUL1)
    conv_scale = (1.0 / math.sqrt(H[0]) / fan, 0.5 / math.sqrt(16.0) / math.sqrt(H[1]) / fan)
    ALPHA, COUNT = FEAT, FEAT + 1

    with ExitStack() as ctx:
        def sb(name, shape, dt=f32):
            return ctx.enter_context(nc.sbuf_tensor(name, shape, dt))

        def sem(name):
            return ctx.enter_context(nc.semaphore(name))

        acc = sb("acc", [P, BLOCKS, n_rows])
        first_i = sb("first_i", [P, n_chunks], i32)
        first_f = sb("first_f", [P, n_chunks])
        dst_i = sb("dst_i", [P, n_chunks * TILES], i32)
        dst_rel = sb("dst_rel", [P, n_chunks * TILES])
        dst_out = sb("dst_out", [P, n_chunks * TILES])
        n_inside = sb("n_inside", [P, 1])
        ones = sb("ones", [P, 1])
        n_outside = sb("n_outside", [1, 1], i32)
        gen_iota = sb("gen_iota", [P, WIN])
        node_a = sb("node_a", [P, n_ntiles])
        iota_i = sb("iota_i", [P, WIN], i32)
        iota = sb("iota", [P, WIN])
        row_i = sb("row_i", [P, P], i32)
        ident = sb("ident", [P, P])
        zeros = sb("zeros", [P, BLOCKS, P])
        eps = sb("eps", [P, 1])
        fc1w = [sb("fc1w0", [P, 2 * H[0]]), sb("fc1w1", [P, H[1]])]
        fc2w = [sb("fc2w0", [P, 2, WNUM]), sb("fc2w1", [H[1], 1, WNUM])]
        nodew = [sb(f"nodew{l}", [P, 2, FEAT]) for l in range(2)]
        convw = [sb(f"convw{l}", [P, 2, FEAT + 2]) for l in range(2)]
        yz_cols = COUNT + 1 - MUL0
        convyz = [sb(f"convyz{l}", [P, 2, yz_cols]) for l in range(2)]
        attr = sb("attr", [P, SLOTS, CHUNK])
        src = sb("src", [P, SLOTS, TILES], i32)
        sph = sb("sph", [P, SLOTS, TILES, SPH])
        rows = sb("rows", [P, SLOTS, TILES, FEAT])
        hidden = sb("hidden", [P, 2, CHUNK])
        hot = sb("hot", [P, 2, TILES, SPH + 1, WIN])
        sh_vec = sb("sh_vec", [P, 2, TILES, VEC, MUL1])
        sh_dot = sb("sh_dot", [P, 2, TILES, MUL1])
        prod = sb("prod", [P, 2, TILES, PROD])
        inside = prod[:, :, :, :].rearrange("p k t n -> p (k t n)")[:, 0:n_chunks * TILES]
        x_t = sb("x_t", [P, 2, 2, 2 * P])
        quad_t = prod[:, :, :, :].rearrange("p k t n -> p (k t n)")[:, 0:2 * 2 * QUAD].rearrange(
            "p (k s e) -> p k s e", k=2, s=2)
        quad_row = rows[:, 0:2, :, :]
        x_row = sb("x_row", [P, 4, FEAT])
        maps = sb("maps", [P, 4, 2, FEAT])
        res_out = sb("res_out", [P, 4, FEAT])
        res_in = sb("res_in", [P, 4, FEAT])
        sums = sb("sums", [P, 2, BLOCKS, P])
        mixed = sb("mixed", [P, 4, FEAT])
        count1, per_count, scaled, gate = (sb(f"small{i}", [P, 4]) for i in range(4))
        bn = sb("bn", [P, 4, 6])
        mean_var = sb("mean_var", [P, 4, 2])
        std, rstd = sb("std", [P, 4]), sb("rstd", [P, 4])

        bank = [ctx.enter_context(nc.psum_tensor(f"bank{b}", [P, BANK], f32)) for b in range(8)]
        hid_ps, w_ps, win_ps = bank[0:2], bank[2:6], bank[6:8]
        conv_ps, trans_ps, map_ps = bank[0:2] + bank[6:8], bank[2:4], bank[4:6]

        nodew_zeroed, nodew_in, nodew_ready = sem("nodew_zeroed"), sem("nodew_in"), sem("nodew_ready")
        index_in, weights_zeroed, weights_in = sem("index_in"), sem("weights_zeroed"), sem("weights_in")
        node_a_in, weights_ready = sem("node_a_in"), sem("weights_ready")
        iota_made, consts_made, acc_zeroed = sem("iota_made"), sem("consts_made"), sem("acc_zeroed")
        attr_zeroed = sem("attr_zeroed")
        prep_step = sem("prep_step")
        attr_in = [sem(f"attr_in{k}") for k in range(SLOTS)]
        src_in = [sem(f"src_in{k}") for k in range(SLOTS)]
        sph_in = [sem(f"sph_in{k}") for k in range(SLOTS)]
        rows_in = [sem(f"rows_in{k}") for k in range(SLOTS)]
        fc1_done, hidden_ready = sem("fc1_done"), sem("hidden_ready")
        w_ready, prod_done = sem("w_ready"), sem("prod_done")
        hot_made, hot_ready = sem("hot_made"), sem("hot_ready")
        vec_made, dot_made = sem("vec_made"), sem("dot_made")
        summed, acc_added = sem("summed"), sem("acc_added")
        counted, outside_ready = sem("counted"), sem("outside_ready")
        total_done = sem("total_done")
        gen_loaded, gen_rows = sem("gen_loaded"), sem("gen_rows")
        gen_fc1, gen_hidden, gen_w, gen_prod = sem("gen_fc1"), sem("gen_hidden"), sem("gen_w"), sem("gen_prod")
        gen_hot, gen_summed, gen_added, gen_step = sem("gen_hot"), sem("gen_summed"), sem("gen_added"), sem("gen_step")
        quad_t_in = [sem(f"quad_t_in{j}") for j in range(2)]
        quad_row_in = [sem(f"quad_row_in{j}") for j in range(2)]
        res_in_sem = [sem(f"res_in_sem{j}") for j in range(2)]
        tab_stored = [sem(f"tab_stored{j}") for j in range(2)]
        row_stored = [sem(f"row_stored{j}") for j in range(2)]
        node_mm, maps_ready, res_ready = sem("node_mm"), sem("maps_ready"), sem("res_ready")
        sums_staged, conv_done, stats_done = sem("sums_staged"), sem("conv_done"), sem("stats_done")
        count1_made, per_count_made, scaled_made = sem("count1_made"), sem("per_count_made"), sem("scaled_made")
        gate_made, mixed_ready, bn_made = sem("gate_made"), sem("mixed_ready"), sem("bn_made")
        std_done, rstd_made, normed = sem("std_done"), sem("rstd_made"), sem("normed")
        transposed, xt_copied = sem("transposed"), sem("xt_copied")
        turn = {e: sem(f"turn_{e}") for e in ("sp", "pool", "act", "dve", "pe")}

        def reached(n, least):
            return not isinstance(n, int) or n >= least

        def in_range(n, count):
            return not isinstance(n, int) or 0 <= n < count

        def chunk_no(l, c):
            return l * n_chunks + c

        def slot_loads(g, k, each=16):
            return (each // SLOTS) * (g - k) + each

        def tile_no(phase, n):
            return phase * n_ntiles + n

        def pairs_before(number, q, each=16):
            return each // 4 * (number - q)

        def pipeline(eng, step, count, peel, lag):
            for n in range(peel):
                step(n, n % 4)
            with eng.Fori(peel // 4, count // 4) as i:
                for k in range(4):
                    step(i * 4 + k, k)
            for n in range(count, count + lag):
                step(n, n % 4)

        def over_octets(eng, step, lag):
            peel = 8 + n_ntiles % 8
            for n in range(peel):
                step(n, n % 8)
            with eng.Fori(0, (n_ntiles - peel) // 8) as i:
                for k in range(8):
                    step(i * 8 + (peel + k), (peel + k) % 8)
            for n in range(n_ntiles, n_ntiles + lag):
                step(n, n % 8)

        def quads_in(n, q):
            return (n - q) * 2 + 16

        def over_chunks(eng, step, lag):
            pipeline(eng, step, n_chunks, 4, lag)

        def over_tiles(eng, step, lag):
            pipeline(eng, step, n_ntiles, 8, lag)

        def in_general(eng, l, step):
            eng.wait_ge(outside_ready, 1)
            outside = eng.value_load(n_outside[0:1, 0:1], min_val=0, max_val=n_slots)
            with eng.If(outside > 0):
                with eng.Fori(0, n_chunks) as c:
                    step(c, chunk_no(l, c))

        def over_windows(eng, g, step):
            first = held(eng, g * n_windows)
            with eng.Fori(0, n_windows) as v:
                step(v, first + v)

        def held(eng, value):
            return value if isinstance(value, int) else eng.snap(value)

        def nodew_loads(l):
            out = []
            for s, (w0, w1) in enumerate((("t0", "t1"), ("s0", "s1"))):
                out.append((nodew[l][0:MUL0, s, 0:MUL0], d[f"L{l}_{w0}"]))
                for m in range(VEC):
                    out.append((nodew[l][32 * m:32 * m + 32, s, MUL0 + 32 * m:MUL0 + 32 * m + 32], d[f"L{l}_{w1}"]))
            return out

        def weight_loads(l):
            w = {k: d[f"L{l}_{k}"] for k in ("fc1", "fc2", "a", "b", "c", "dd")}
            out = []
            for b in range(2 - l):
                out.append((fc1w[l][K1[l] * b:K1[l] * (b + 1), H[l] * b:H[l] * (b + 1)], w["fc1"]))
                out.append((fc2w[l][H[l] * b:H[l] * (b + 1), b, :], w["fc2"]))
            for m in range(VEC):
                out.append((convw[l][32 * m:32 * m + 32, 0, MUL0 + 32 * m:MUL0 + 32 * m + 32], w["c"]))
            out.append((convw[l][96:128, 0, 0:MUL0], w["dd"]))
            out.append((convw[l][0:MUL0, 1, 0:MUL0], w["a"]))
            out.append((convw[l][MUL0:P, 1, MUL0:MUL0 + MUL1], w["b"]))
            if l == 0:
                out.append((convw[l][96:128, 0, ALPHA:ALPHA + 1], d["L0_alpha"][MUL0:MUL0 + MUL1, :]))
                out.append((convw[l][0:MUL0, 1, ALPHA:ALPHA + 1], d["L0_alpha"][0:MUL0, :]))
            return out
        loads = weight_loads(0) + nodew_loads(1) + weight_loads(1)
        n_weight_loads = len(loads)
        pair_rows = "(t p) f -> p t f"

        block = ctx.enter_context(nc.Block())

        @block.sync
        def _(sp):
            sp.wait_ge(nodew_zeroed, 1)
            for dst, source in nodew_loads(0):
                sp.dma_start(dst, source).then_inc(nodew_in, 16)
            sp.dma_start(node_a[:, :], d["node_a"]).then_inc(node_a_in, 16)

            def store_maps(phase, n, q):
                at = bass.ds(held(sp, n * P - P), 2 * P)
                sp.wait_ge(maps_ready, tile_no(phase, n) + 1)
                sp.sem_inc(turn["sp"])
                sp.dma_start(d[f"table{phase}"][at, :].rearrange(pair_rows, p=P),
                             maps[:, q - 1:q + 1, 0, :]).then_inc(tab_stored[q // 2], 16)
                sp.wait_ge(res_ready, tile_no(phase, n) + 1)
                sp.sem_inc(turn["sp"])
                sp.dma_start(d[f"resid{phase}"][at, :].rearrange(pair_rows, p=P),
                             res_out[:, q - 1:q + 1, :]).then_inc(row_stored[q // 2], 16)

            def pre_step(n, q):
                if q % 4 == 0 and in_range(n, n_ntiles):
                    at, slot = bass.ds(held(sp, n * P), QUAD), q // 4
                    if reached(n, 8):
                        sp.wait_ge(node_mm, n - 4)
                        sp.sem_inc(turn["sp"])
                    sp.dma_start(quad_t[0:VEC * MUL1, slot, :, :], d["xt"][:, :, at]).then_inc(quad_t_in[slot], 16)
                    if reached(n, 8):
                        sp.wait_ge(res_ready, n - 4)
                        sp.sem_inc(turn["sp"])
                    sp.dma_start(quad_row[:, slot, :, :], d["x"][at, :].rearrange(pair_rows, p=P)
                                 ).then_inc(quad_row_in[slot], 16)
                if q % 2 == 0 and in_range(n - 3, n_ntiles):
                    store_maps(0, n - 3, (q - 3) % 4)
            over_octets(sp, pre_step, 4)
            sp.wait_ge(attr_zeroed, 1)

            def edge_loads(l, at, k):
                one = bass.ds(at, 1)
                return ((attr[0:(2 - l) * K1[l], k, 0:COLS[l]],
                         d[f"attr{l}"][one, :, :].rearrange("o k e -> (o k) e")),
                        (src[:, k, :], d["src"][one, :, :].rearrange("o p t -> (o p) t")),
                        (sph[:, k, :, :].rearrange("p t m -> p (t m)"),
                         d["sph"][one, :, :].rearrange("o p e -> (o p) e")))

            def load_edges(l, c, k):
                g = chunk_no(l, c)
                at = held(sp, c)
                if reached(g, SLOTS):
                    sp.wait_ge(fc1_done, g - 3)
                    sp.sem_inc(turn["sp"])
                loads_of = edge_loads(l, at, k)
                sp.dma_start(*loads_of[0]).then_inc(attr_in[k], 16)
                if reached(g, SLOTS):
                    sp.wait_ge(rows_in[k], slot_loads(g - SLOTS, k, 16 * TILES))
                    sp.sem_inc(turn["sp"])
                sp.dma_start(*loads_of[1]).then_inc(src_in[k], 16)
                if reached(g, SLOTS):
                    sp.wait_ge(hot_ready, g - 3)
                    sp.sem_inc(turn["sp"])
                sp.dma_start(*loads_of[2]).then_inc(sph_in[k], 16)

            for l in range(2):
                over_chunks(sp, lambda c, k: load_edges(l, c, k), 0)
                sp.wait_ge(acc_added, chunk_no(l + 1, 0))

                def general(c, g):
                    at = held(sp, c)
                    sp.wait_ge(gen_added, g * n_windows + 1)
                    sp.sem_inc(turn["sp"])
                    for dst, source in edge_loads(l, at, 0):
                        sp.dma_start(dst, source).then_inc(gen_loaded, 16)
                in_general(sp, l, general)
                lag = (7, 5)[l]
                for s in range(2):
                    sp.wait_ge(row_stored[s], pairs_before(tile_no(l + 1, 0), 0))

                def node_step(n, j):
                    if j % 2 == 1:
                        return
                    if in_range(n, n_ntiles):
                        at = bass.ds(held(sp, n * P), 2 * P)
                        if reached(tile_no(l, n), 4):
                            sp.wait_ge(mixed_ready, tile_no(l, n) - 2)
                            sp.sem_inc(turn["sp"])
                        sp.dma_start(res_in[:, j:j + 2, :], d[f"resid{l}"][at, :].rearrange(pair_rows, p=P)
                                     ).then_inc(res_in_sem[j // 2], 16)
                    if in_range(n - lag, n_ntiles):
                        q = (j - lag) % 4
                        if l == 0:
                            store_maps(1, n - lag, q)
                        else:
                            at = bass.ds(held(sp, n * P - 6 * P), 2 * P)
                            sp.wait_ge(normed, tile_no(1, n - 5) + 1)
                            sp.sem_inc(turn["sp"])
                            sp.dma_start(d["out"][at, :].rearrange(pair_rows, p=P),
                                         x_row[:, q - 1:q + 1, :]).then_inc(row_stored[q // 2], 16)
                over_tiles(sp, node_step, lag)
            for s in range(2):
                sp.wait_ge(row_stored[s], pairs_before(tile_no(3, 0), 0))
                sp.wait_ge(tab_stored[s], pairs_before(tile_no(2, 0), 0))

        @block.gpsimd
        def _(pool):
            nc.gpsimd.iota(iota_i[:, :], pattern=[[1, WIN]], base=0, channel_multiplier=0).then_inc(iota_made, 1)
            nc.gpsimd.iota(row_i[:, :], pattern=[[1, P]], base=0, channel_multiplier=-1).then_inc(iota_made, 1)
            pool.wait_ge(weights_zeroed, 7)
            pool.dma_start(dst_i[:, :], d["dst"]).then_inc(index_in, 16)
            pool.dma_start(first_i[:, :], d["first"].partition_broadcast(P)).then_inc(index_in, 16)
            for dst, source in loads:
                pool.dma_start(dst, source).then_inc(weights_in, 16)
            nc.gpsimd.memset(attr[:, :, :], 0.0).then_inc(attr_zeroed, 1)
            nc.gpsimd.memset(acc[:, :, :], 0.0).then_inc(acc_zeroed, 1)
            nc.gpsimd.memset(zeros[:, :, :], 0.0).then_inc(consts_made, 1)

            def gather_tile(l, k, t):
                return nc.gpsimd.indirect_dma_start(
                    out=rows[:, k, t, :], out_offset=None, in_=d[f"table{l}"],
                    in_offset=bass.IndirectOffsetOnAxis(ap=src[:, k, t:t + 1], axis=0))

            def gather(l, c, k):
                g = chunk_no(l, c)
                if reached(g, SLOTS):
                    pool.wait_ge(prod_done, 2 * (g - 3))
                pool.wait_ge(src_in[k], slot_loads(g, k))
                pool.sem_inc(turn["pool"])
                for t in range(TILES):
                    gather_tile(l, k, t).then_inc(rows_in[k], 16)

            for l in range(2):
                for s in range(2):
                    pool.wait_ge(tab_stored[s], pairs_before(tile_no(l + 1, 0), 0))
                if l == 0:
                    pool.wait_ge(res_ready, n_ntiles)
                over_chunks(pool, lambda c, k: gather(l, c, k), 0)

                def general(c, g):
                    pool.wait_ge(gen_loaded, 48 * (g + 1))
                    pool.sem_inc(turn["pool"])
                    for t in range(TILES):
                        gather_tile(l, 0, t).then_inc(gen_rows, 16)
                in_general(pool, l, general)
                if l == 0:
                    pool.wait_ge(consts_made, 2)

                    def clear(n, j):
                        at = held(pool, n * P)
                        pool.wait_ge(sums_staged, n + 1)
                        pool.sem_inc(turn["pool"])
                        nc.gpsimd.tensor_copy(acc[:, :, bass.ds(at, P)], zeros[:, :, :]).then_inc(acc_zeroed, 1)
                    over_tiles(pool, clear, 0)

        @block.scalar
        def _(act):
            act.wait_ge(node_a_in, 16)

            def maps_out(phase, n, q):
                number, at = tile_no(phase, n), held(act, n)
                act.wait_ge(node_mm, number + 1)
                if reached(number, 4):
                    act.wait_ge(res_ready, number - 3)
                    act.wait_ge(tab_stored[q // 2], pairs_before(number, q))
                    act.sem_inc(turn["act"])
                nc.scalar.activation(maps[:, q, :, :].rearrange("p s f -> p (s f)"), map_ps[q % 2][:, 0:2 * FEAT],
                                     ACT.Copy, scale=node_a[:, bass.ds(at, 1)]).then_inc(maps_ready, 1)
            over_tiles(act, lambda n, q: maps_out(0, n, q), 0)

            def hidden_act(l, c, k):
                g = chunk_no(l, c)
                act.wait_ge(fc1_done, g + 1)
                if reached(g, 2):
                    act.wait_ge(w_ready, 2 * (g - 1))
                activate(l, k).then_inc(hidden_ready, 1)

            def activate(l, k):
                n = H[l] * (2 - l)
                return nc.scalar.activation(hidden[0:n, k % 2, 0:COLS[l]], hid_ps[k % 2][0:n, 0:COLS[l]], h_func[l],
                                            scale=h_scale[l])

            def node_step(l, n, q):
                j = q % 2
                if in_range(n, n_ntiles):
                    at, number = held(act, n * P), tile_no(l, n)
                    if reached(number, 2):
                        act.wait_ge(conv_done, number - 1)
                        act.sem_inc(turn["act"])
                    nc.scalar.copy(sums[:, j, :, :], acc[:, :, bass.ds(at, P)]).then_inc(sums_staged, 1)
                if in_range(n - 3, n_ntiles):
                    q3 = (q - 3) % 4
                    act.wait_ge(stats_done, tile_no(l, n - 3) + 1)
                    nc.scalar.activation(std[:, q3:q3 + 1], mean_var[:, q3, 1:2], ACT.Sqrt,
                                         bias=eps[:, 0:1]).then_inc(std_done, 1)
                if l == 0 and in_range(n - 6, n_ntiles):
                    maps_out(1, n - 6, (q - 2) % 4)
                if l == 0 and in_range(n - 5, n_ntiles):
                    act.wait_ge(transposed, n - 4)
                    if reached(n, 9):
                        act.wait_ge(node_mm, tile_no(1, n - 9) + 1)
                        act.sem_inc(turn["act"])
                    q1 = (q - 1) % 4
                    tile_t, ps = x_t[:, q1 // 2, :, q1 % 2 * P:q1 % 2 * P + P], trans_ps[1 - j]
                    nc.scalar.copy(tile_t[0:MUL0, 0, :], ps[0:MUL0, 0:P])
                    nc.scalar.copy(tile_t[0:VEC * MUL1, 1, :], ps[0:VEC * MUL1, P:2 * P]).then_inc(xt_copied, 1)

            act.wait_ge(consts_made, 2)
            for l in range(2):
                over_chunks(act, lambda c, k: hidden_act(l, c, k), 0)
                act.wait_ge(acc_added, chunk_no(l + 1, 0))

                def general(c, g):
                    all_added = held(act, (g + 1) * n_windows + 1)
                    act.wait_ge(gen_fc1, g + 1)
                    activate(l, 0).then_inc(gen_hidden, 1)
                    act.wait_ge(gen_added, all_added)
                in_general(act, l, general)
                over_tiles(act, lambda n, q: node_step(l, n, q), 6 if l == 0 else 3)

        @block.vector
        def _(dve):
            steps = [0]

            def own(ins):
                steps[0] += 1
                ins.then_inc(prep_step, 1)
                dve.wait_ge(prep_step, steps[0])

            nc.vector.memset(nodew[0][:, :, :], 0.0).then_inc(nodew_zeroed, 1)
            nc.vector.memset(quad_t[VEC * MUL1:P, :, :, :], 0.0)
            nc.vector.memset(nodew[1][:, :, :], 0.0).then_inc(weights_zeroed, 1)
            for l in range(2):
                nc.vector.memset(convw[l][:, :, :], 0.0).then_inc(weights_zeroed, 1)
                nc.vector.memset(fc1w[l][:, :], 0.0).then_inc(weights_zeroed, 1)
                nc.vector.memset(fc2w[l][:, :, :], 0.0).then_inc(weights_zeroed, 1)
            nc.vector.memset(x_t[:, :, :, :], 0.0)
            for l in range(2):
                nc.vector.memset(convyz[l][:, :, :], 0.0)
            nc.vector.memset(ones[:, :], 1.0)
            nc.vector.memset(eps[:, :], LN_EPS).then_inc(consts_made, 1)
            dve.sem_inc(gen_added)

            def scale_nodew(l):
                nc.vector.tensor_scalar(nodew[l][:, :, 0:MUL0], nodew[l][:, :, 0:MUL0],
                                        1.0 / math.sqrt(MUL0), None, ALU.mult)
                return nc.vector.tensor_scalar(nodew[l][:, :, MUL0:FEAT], nodew[l][:, :, MUL0:FEAT],
                                               1.0 / math.sqrt(MUL1), None, ALU.mult)
            dve.wait_ge(nodew_in, 16 * len(nodew_loads(0)))
            scale_nodew(0).then_inc(nodew_ready, 1)

            def before_edges():
                dve.wait_ge(iota_made, 2)
                nc.vector.tensor_copy(iota[:, :], iota_i[:, :])
                own(nc.vector.tensor_scalar(ident[:, :], row_i[:, :], 0.0, None, ALU.is_equal))
                dve.wait_ge(index_in, 32)
                nc.vector.tensor_copy(dst_out[:, :], dst_i[:, :])
                own(nc.vector.tensor_copy(first_f[:, :], first_i[:, :]))
                own(nc.vector.tensor_tensor(
                    dst_rel[:, :].rearrange("p (c t) -> p c t", t=TILES),
                    dst_out[:, :].rearrange("p (c t) -> p c t", t=TILES),
                    first_f[:, :].unsqueeze(2).broadcast_to([P, n_chunks, TILES]), ALU.subtract))
                own(nc.vector.tensor_scalar(inside, dst_rel[:, :], float(WIN), None, ALU.is_lt))
                own(nc.vector.scalar_tensor_tensor(out=inside, in0=dst_rel[:, :], scalar=0.0,
                                                   in1=inside, op0=ALU.is_ge, op1=ALU.mult))
                nc.vector.tensor_reduce(n_inside[:, :], inside, AX.X, ALU.add).then_inc(counted, 1)
                own(nc.vector.scalar_tensor_tensor(out=dst_out[:, :], in0=inside,
                                                   scalar=-float(2 * n_rows), in1=dst_out[:, :],
                                                   op0=ALU.mult, op1=ALU.add))
                dve.wait_ge(total_done, 1)
                nc.vector.tensor_scalar(n_outside[:, :], bank[7][0:1, 0:1], -1.0, float(n_slots),
                                        ALU.mult, ALU.add).then_inc(outside_ready, 1)
                dve.wait_ge(weights_in, 16 * n_weight_loads)
                third = 1.0 / math.sqrt(VEC)
                own(scale_nodew(1))
                for l in range(2):
                    own(nc.vector.tensor_scalar(convw[l][:, :, :], convw[l][:, :, :], conv_scale[l], None, ALU.mult))
                    own(nc.vector.tensor_scalar(convw[l][96:128, 0, 0:MUL0], convw[l][96:128, 0, 0:MUL0],
                                                third, None, ALU.mult))
                    for m in (1, 2):
                        nc.vector.tensor_copy(convyz[l][MUL0:P, m - 1, m * MUL1:(m + 1) * MUL1],
                                              convw[l][MUL0:P, 1, MUL0:MUL0 + MUL1])
                nc.vector.tensor_copy(convyz[0][0:MUL0, 0, yz_cols - 1:yz_cols], ident[0:MUL0, 0:1])
                nc.vector.tensor_scalar(convw[0][96:128, 0, ALPHA:ALPHA + 1], convw[0][96:128, 0, ALPHA:ALPHA + 1],
                                        third, None, ALU.mult).then_inc(weights_ready, 1)

            def resid_out(phase, n, q, row):
                number = tile_no(phase, n)
                dve.wait_ge(maps_ready, number + 1)
                if reached(number, 4):
                    dve.wait_ge(row_stored[q // 2], pairs_before(number, q))
                nc.vector.tensor_tensor(res_out[:, q, :], maps[:, q, 1, :], row, ALU.add).then_inc(res_ready, 1)

            def pre_step(n, q):
                dve.wait_ge(quad_row_in[q // 4], quads_in(n, q))
                resid_out(0, n, q % 4, quad_row[:, q // 4, q % 4, :])
            over_octets(dve, pre_step, 0)
            before_edges()

            def spread_hot(k):
                return nc.vector.tensor_tensor(
                    hot[:, k % 2, :, 0:SPH, :],
                    hot[:, k % 2, :, SPH:SPH + 1, :].broadcast_to([P, TILES, SPH, WIN]),
                    sph[:, k, :, :].unsqueeze(3).broadcast_to([P, TILES, SPH, WIN]), ALU.mult)

            def sh_times(k):
                return nc.vector.tensor_tensor(
                    sh_vec[:, k % 2, :, :, :], rows[:, k, :, MUL0:FEAT].rearrange("p t (m u) -> p t m u", m=VEC),
                    sph[:, k, :, 1:SPH].unsqueeze(3).broadcast_to([P, TILES, VEC, MUL1]), ALU.mult)

            def sh_sum(k):
                return nc.vector.tensor_reduce(sh_dot[:, k % 2, :, :],
                                               sh_vec[:, k % 2, :, :, :].rearrange("p t m u -> p t u m"),
                                               AX.X, ALU.add)

            def windows(l, c, k):
                g, at = chunk_no(l, c), held(dve, c * TILES)
                if reached(g, 2):
                    dve.wait_ge(summed, g - 1)
                    dve.sem_inc(turn["dve"])
                nc.vector.tensor_tensor(
                    hot[:, k % 2, :, SPH, :], iota[:, :].unsqueeze(1).broadcast_to([P, TILES, WIN]),
                    dst_rel[:, bass.ds(at, TILES)].unsqueeze(2).broadcast_to([P, TILES, WIN]),
                    ALU.is_equal).then_inc(hot_made, 1)
                dve.wait_ge(rows_in[k], slot_loads(g, k, 16 * TILES))
                dve.wait_ge(sph_in[k], slot_loads(g, k))
                sh_times(k).then_inc(vec_made, 1)
                dve.wait_ge(hot_made, g + 1)
                spread_hot(k).then_inc(hot_ready, 1)
                dve.wait_ge(vec_made, g + 1)
                sh_sum(k).then_inc(dot_made, 1)

            def multiply(k, q):
                w = w_ps[2 * (k % 2) + q][:, 0:2 * WNUM].rearrange("p (t n) -> p t n", t=2)
                out = prod[:, k % 2, 2 * q:2 * q + 2, :]
                row = rows[:, k, 2 * q:2 * q + 2, :]
                nc.vector.tensor_tensor(
                    out[:, :, 0:C_AT].rearrange("p t (s u) -> p t s u", s=2),
                    w[:, :, 0:2 * MUL0].rearrange("p t (s u) -> p t s u", s=2),
                    row[:, :, 0:MUL0].unsqueeze(2).broadcast_to([P, 2, 2, MUL0]), ALU.mult)
                nc.vector.tensor_tensor(
                    out[:, :, C_AT:D_AT].rearrange("p t (m u) -> p t m u", m=VEC),
                    w[:, :, C_AT:C_AT + MUL1].unsqueeze(2).broadcast_to([P, 2, VEC, MUL1]),
                    row[:, :, MUL0:FEAT].rearrange("p t (m u) -> p t m u", m=VEC), ALU.mult)
                return nc.vector.tensor_tensor(out[:, :, D_AT:PROD], w[:, :, C_AT + MUL1:WNUM],
                                               sh_dot[:, k % 2, 2 * q:2 * q + 2, :], ALU.mult)

            def products(l, c, k):
                g = chunk_no(l, c)
                dve.wait_ge(dot_made, g + 1)
                for q in range(2):
                    dve.wait_ge(w_ready, 2 * g + q + 1)
                    multiply(k, q).then_inc(prod_done, 1)

            def add_window(l, k, nodes):
                ps = win_ps[k % 2]
                nc.vector.tensor_tensor(acc[0:MUL0, 0, nodes], acc[0:MUL0, 0, nodes], ps[0:MUL0, 0:WIN], ALU.add)
                nc.vector.tensor_tensor(acc[MUL0:P, 0:VEC, nodes], acc[MUL0:P, 0:VEC, nodes],
                                        ps[MUL0:P, WIN:SPH * WIN].rearrange("p (m w) -> p m w", m=VEC), ALU.add)
                if l == 0:
                    nc.vector.tensor_tensor(acc[0:1, 1, nodes], acc[0:1, 1, nodes],
                                            ps[0:1, COUNT_COLS:COUNT_COLS + WIN], ALU.add)
                return nc.vector.tensor_tensor(acc[:, VEC, nodes], acc[:, VEC, nodes],
                                               ps[:, CD_COLS:COUNT_COLS], ALU.add)

            def add_sums(l, c, k):
                g = chunk_no(l, c)
                at = dve.value_load(first_i[0:1, bass.ds(c, 1)], min_val=0, max_val=n_nodes)
                dve.wait_ge(summed, g + 1)
                if reached(g, 1):
                    dve.wait_ge(acc_added, g)
                    dve.sem_inc(turn["dve"])
                add_window(l, k, bass.ds(at, WIN)).then_inc(acc_added, 1)

            def col(t, q):
                return t[:, q:q + 1]

            def node_step(l, n, q):
                q1, q3, here, ps = (q - 1) % 4, (q - 3) % 4, in_range(n, n_ntiles), conv_ps[q]
                if here:
                    number, at = tile_no(l, n), held(dve, n)
                    dve.wait_ge(conv_done, number + 1)
                    if l == 0:
                        nc.vector.tensor_scalar(col(count1, q), ps[:, COUNT:COUNT + 1], 1.0, None,
                                                ALU.max).then_inc(count1_made, 1)
                if l == 0 and in_range(n - 6, n_ntiles):
                    q2 = (q - 2) % 4
                    resid_out(1, n - 6, q2, x_row[:, q2, :])
                if here and l == 0:
                    dve.wait_ge(count1_made, n + 1)
                    nc.vector.reciprocal(col(per_count, q), col(count1, q)).then_inc(per_count_made, 1)
                if in_range(n - 3, n_ntiles):
                    dve.wait_ge(std_done, tile_no(l, n - 3) + 1)
                    nc.vector.reciprocal(col(rstd, q3), col(std, q3)).then_inc(rstd_made, 1)
                if here and l == 0:
                    dve.wait_ge(per_count_made, n + 1)
                    dve.sem_inc(turn["dve"])
                    nc.vector.tensor_tensor(col(scaled, q), col(per_count, q), node_a[:, bass.ds(at, 1)],
                                            ALU.mult).then_inc(scaled_made, 1)
                if in_range(n - 1, n_ntiles):
                    dve.wait_ge(mixed_ready, tile_no(l, n - 1) + 1)
                    nc.vector.bn_stats(bn[:, q1, :], mixed[:, q1, :]).then_inc(bn_made, 1)
                if here and l == 0:
                    dve.wait_ge(scaled_made, n + 1)
                    nc.vector.tensor_scalar(col(gate, q), ps[:, ALPHA:ALPHA + 1], col(scaled, q), col(scaled, q),
                                            ALU.mult, ALU.mult).then_inc(gate_made, 1)
                if in_range(n - 3, n_ntiles):
                    if l == 0 and reached(n, 7):
                        dve.wait_ge(transposed, n - 6)
                        dve.wait_ge(res_ready, tile_no(1, n - 7) + 1)
                    if l == 1:
                        dve.wait_ge(row_stored[q3 // 2], pairs_before(tile_no(2, n - 3), q3))
                    dve.wait_ge(rstd_made, tile_no(l, n - 3) + 1)
                    nc.vector.tensor_scalar(x_row[:, q3, :], mixed[:, q3, :], mean_var[:, q3, 0:1], col(rstd, q3),
                                            ALU.subtract, ALU.mult).then_inc(normed, 1)
                if in_range(n - 1, n_ntiles):
                    dve.wait_ge(bn_made, tile_no(l, n - 1) + 1)
                    dve.sem_inc(turn["dve"])
                    nc.vector.bn_aggr(mean_var[:, q1, :], bn[:, q1, :]).then_inc(stats_done, 1)
                if here:
                    if l == 0:
                        dve.wait_ge(gate_made, n + 1)
                    if reached(number, 4):
                        dve.wait_ge(normed, number - 3)
                    dve.wait_ge(res_in_sem[q // 2], pairs_before(number, q) + 16)
                    dve.sem_inc(turn["dve"])
                    nc.vector.scalar_tensor_tensor(
                        out=mixed[:, q, :], in0=ps[:, 0:FEAT],
                        scalar=col(gate, q) if l == 0 else node_a[:, bass.ds(at, 1)],
                        in1=res_in[:, q, :], op0=ALU.mult, op1=ALU.add).then_inc(mixed_ready, 1)

            dve.wait_ge(acc_zeroed, 1)
            for l in range(2):
                def chunk_step(c, k):
                    if in_range(c - 3, n_chunks):
                        add_sums(l, c - 3, (k - 3) % SLOTS)
                    if in_range(c, n_chunks):
                        windows(l, c, k)
                    if in_range(c, n_chunks):
                        products(l, c, k)
                over_chunks(dve, chunk_step, 3)

                def general(c, g):
                    tiles = bass.ds(held(dve, c * TILES), TILES)
                    steps_before = held(dve, g * (3 + 2 * n_windows))
                    dve.wait_ge(gen_loaded, 48 * (g + 1))
                    dve.wait_ge(gen_rows, 16 * TILES * (g + 1))
                    sh_times(0).then_inc(gen_step, 1)
                    dve.wait_ge(gen_step, steps_before + 1)
                    sh_sum(0).then_inc(gen_step, 1)
                    nc.vector.tensor_copy(gen_iota[:, :], iota[:, :]).then_inc(gen_step, 1)
                    dve.wait_ge(gen_w, g + 1)
                    dve.wait_ge(gen_step, steps_before + 3)
                    multiply(0, 0)
                    multiply(0, 1).then_inc(gen_prod, 1)

                    def window(v, number):
                        nodes = bass.ds(held(dve, v * WIN), WIN)
                        before = held(dve, steps_before + (v * 2 + 3))
                        nc.vector.tensor_tensor(
                            hot[:, 0, :, SPH, :], gen_iota[:, :].unsqueeze(1).broadcast_to([P, TILES, WIN]),
                            dst_out[:, tiles].unsqueeze(2).broadcast_to([P, TILES, WIN]),
                            ALU.is_equal).then_inc(gen_step, 1)
                        dve.wait_ge(gen_step, before + 1)
                        nc.vector.tensor_scalar(gen_iota[:, :], gen_iota[:, :], float(WIN), None,
                                                ALU.add).then_inc(gen_step, 1)
                        spread_hot(0).then_inc(gen_hot, 1)
                        dve.wait_ge(gen_step, before + 2)
                        dve.wait_ge(gen_summed, number + 1)
                        add_window(l, 0, nodes).then_inc(gen_added, 1)
                        dve.wait_ge(gen_added, number + 2)
                        dve.sem_inc(turn["dve"])
                    over_windows(dve, g, window)
                in_general(dve, l, general)
                over_tiles(dve, lambda n, q: node_step(l, n, q), 6 if l == 0 else 3)
                if l == 0:
                    dve.wait_ge(acc_zeroed, 1 + n_ntiles)

        @block.tensor
        def _(pe):
            mm = nc.tensor.matmul
            pe.wait_ge(nodew_ready, 1)

            def node_maps(phase, n, q, tile_t):
                number, w, ps = tile_no(phase, n), nodew[phase], map_ps[q % 2][:, 0:2 * FEAT]
                if reached(number, 2):
                    pe.wait_ge(maps_ready, number - 1)
                if phase == 0:
                    pe.wait_ge(quad_t_in[q // 4], quads_in(n, q))
                else:
                    pe.wait_ge(xt_copied, n + 1)
                ps = ps.rearrange("p (s f) -> p s f", s=2)
                mm(ps[:, :, 0:MUL0], tile_t[:, 0, :], w[:, :, 0:MUL0], start=True, stop=True)
                mm(ps[:, :, MUL0:FEAT], tile_t[:, 1, :], w[:, :, MUL0:FEAT],
                   start=True, stop=True).then_inc(node_mm, 1)

            def pre_step(n, q):
                node_maps(0, n, q, quad_t[:, q // 4, :, q % 4 * P:(q % 4 + 1) * P])
            over_octets(pe, pre_step, 0)
            pe.wait_ge(counted, 1)
            mm(bank[7][0:1, 0:1], n_inside[:, :], ones[:, :], start=True, stop=True).then_inc(total_done, 1)
            pe.wait_ge(weights_ready, 1)

            def fc1_mm(l, k):
                n = H[l] * (2 - l)
                return mm(hid_ps[k % 2][0:n, 0:COLS[l]], fc1w[l][:, :], attr[:, k, 0:COLS[l]], start=True, stop=True)

            def fc1(l, c, k):
                g = chunk_no(l, c)
                if reached(g, 2):
                    pe.wait_ge(hidden_ready, g - 1)
                pe.wait_ge(attr_in[k], slot_loads(g, k))
                fc1_mm(l, k).then_inc(fc1_done, 1)

            def fc2_mm(l, k, q):
                ps = w_ps[2 * (k % 2) + q]
                if l == 0:
                    return mm(ps[:, 0:2 * WNUM], hidden[:, k % 2, q * P:(q + 1) * P],
                              fc2w[0][:, :, :].rearrange("p b n -> p (b n)"), start=True, stop=True)
                for t in range(2):
                    e = (2 * q + t) * P
                    last = mm(ps[:, t * WNUM:(t + 1) * WNUM], hidden[0:H[1], k % 2, e:e + P], fc2w[1][:, 0, :],
                              start=True, stop=True)
                return last

            def fc2(l, c, k):
                g = chunk_no(l, c)
                pe.wait_ge(hidden_ready, g + 1)
                for q in range(2):
                    if reached(g, 2):
                        pe.wait_ge(prod_done, 2 * (g - 2) + q + 1)
                    fc2_mm(l, k, q).then_inc(w_ready, 1)

            def sum_mm(l, k):
                ps = win_ps[k % 2]
                for t in range(TILES):
                    p, h, last = prod[:, k % 2, t, :], hot[:, k % 2, t, :, :], t == TILES - 1
                    mm(ps[:, 0:CD_COLS], p[:, 0:C_AT], h[:, 0:SPH, :].rearrange("p b w -> p (b w)"),
                       start=(t == 0), stop=last, skip_group_check=True)
                    if l == 0:
                        mm(ps[0:1, COUNT_COLS:COUNT_COLS + WIN], ones[:, :], h[:, SPH, :],
                           start=False, stop=last, skip_group_check=True)
                    mm(ps[0:D_AT - C_AT, CD_COLS:COUNT_COLS], p[:, C_AT:D_AT], h[:, 0, :],
                       start=False, stop=last, skip_group_check=True)
                    done = mm(ps[D_AT - C_AT:P, CD_COLS:COUNT_COLS], p[:, D_AT:PROD], h[:, SPH, :],
                              start=False, stop=last, skip_group_check=True)
                return done

            def sum_edges(l, c, k):
                g = chunk_no(l, c)
                if reached(g, 2):
                    pe.wait_ge(acc_added, g - 1)
                pe.wait_ge(hot_ready, g + 1)
                pe.wait_ge(prod_done, 2 * g + 2)
                sum_mm(l, k).then_inc(summed, 1)

            def conv(l, n, q):
                number, ps, w, cols, j = tile_no(l, n), conv_ps[q], convw[l], COUNT + 1, q % 2
                if reached(number, 4):
                    pe.wait_ge(mixed_ready, number - 3)
                pe.wait_ge(sums_staged, number + 1)
                mm(ps[:, 0:cols], sums[:, j, 3, :], w[:, 0, 0:cols], start=True, stop=False, skip_group_check=True)
                mm(ps[:, 0:cols], sums[:, j, 0, :], w[:, 1, 0:cols], start=False, stop=False, skip_group_check=True)
                for m in (1, 2):
                    last = mm(ps[:, MUL0:MUL0 + yz_cols], sums[:, j, m, :], convyz[l][:, m - 1, :],
                              start=False, stop=(m == 2), skip_group_check=True)
                last.then_inc(conv_done, 1)

            def transpose(n, q):
                j = q % 2
                if reached(n, 2):
                    pe.wait_ge(xt_copied, n - 1)
                pe.wait_ge(normed, n + 1)
                pe.sem_inc(turn["pe"])
                nc.tensor.transpose(trans_ps[j][0:MUL0, 0:P], x_row[:, q, 0:MUL0], ident[:, :])
                nc.tensor.transpose(trans_ps[j][0:VEC * MUL1, P:2 * P], x_row[:, q, MUL0:FEAT],
                                    ident[:, :]).then_inc(transposed, 1)

            def node_step(l, n, q):
                if in_range(n, n_ntiles):
                    conv(l, n, q)
                if l == 0 and in_range(n - 4, n_ntiles):
                    transpose(n - 4, q)
                if l == 0 and in_range(n - 5, n_ntiles):
                    q1 = (q - 1) % 4
                    node_maps(1, n - 5, q1, x_t[:, q1 // 2, :, q1 % 2 * P:q1 % 2 * P + P])

            for l in range(2):
                def chunk_step(c, k):
                    if in_range(c, n_chunks):
                        fc1(l, c, k)
                    if in_range(c - 1, n_chunks):
                        fc2(l, c - 1, (k - 1) % SLOTS)
                    if in_range(c - 2, n_chunks):
                        sum_edges(l, c - 2, (k - 2) % SLOTS)
                over_chunks(pe, chunk_step, 2)

                def general(c, g):
                    pe.wait_ge(gen_loaded, 48 * (g + 1))
                    fc1_mm(l, 0).then_inc(gen_fc1, 1)
                    pe.wait_ge(gen_hidden, g + 1)
                    fc2_mm(l, 0, 0)
                    fc2_mm(l, 0, 1).then_inc(gen_w, 1)
                    pe.wait_ge(gen_prod, g + 1)
                    pe.sem_inc(turn["pe"])

                    def window(v, number):
                        pe.wait_ge(gen_hot, number + 1)
                        pe.wait_ge(gen_added, number + 1)
                        sum_mm(l, 0).then_inc(gen_summed, 1)
                    over_windows(pe, g, window)
                in_general(pe, l, general)
                over_tiles(pe, lambda n, q: node_step(l, n, q), 5 if l == 0 else 0)


def kernel(**inputs):
    import numpy as np
    import concourse.bacc as bacc
    from concourse import mybir as mb
    from concourse.bass_utils import run_bass_kernel_spmd

    a = {k: np.asarray(v) for k, v in inputs.items()}
    n_nodes, n_edges = a["x"].shape[0], a["src"].shape[0]
    n_chunks = -(-n_edges // (CHUNK * SLOTS)) * SLOTS
    n_ntiles = -(-(n_nodes + 1 + WIN) // (4 * P)) * 4
    n_rows, pad = n_ntiles * P, n_chunks * CHUNK - n_edges

    def component_major(x):
        return x.reshape(-1, MUL1, VEC).transpose(0, 2, 1).reshape(-1, VEC * MUL1)

    x = np.zeros((n_rows, FEAT), a["x"].dtype)
    x[:n_nodes, :MUL0] = a["x"][:, :MUL0]
    x[:n_nodes, MUL0:] = component_major(a["x"][:, MUL0:])
    xt = np.zeros((VEC * MUL1, 2, n_rows), x.dtype)
    xt[:MUL0, 0], xt[:, 1] = x[:, :MUL0].T, x[:, MUL0:].T
    node_a = np.zeros((n_rows, 1), a["node_vec1"].dtype)
    node_a[:n_nodes] = a["node_vec1"]
    src = np.concatenate([a["src"], np.zeros(pad, a["src"].dtype)]).reshape(n_chunks, TILES, P)
    dst = np.concatenate([a["dst"], np.full(pad, n_nodes, a["dst"].dtype)]).reshape(n_chunks, TILES, P)

    def edges(v):
        return np.concatenate([v, np.zeros((pad, v.shape[1]), v.dtype)]).reshape(n_chunks, TILES, P, v.shape[1])
    arrays = {
        "x": x, "xt": xt,
        "node_a": node_a.reshape(n_ntiles, P).T,
        "src": src.transpose(0, 2, 1),
        "dst": dst.transpose(2, 0, 1).reshape(P, n_chunks * TILES),
        "first": dst[:, 0, 0],
        "sph": edges(a["edge_attr_4"]).transpose(0, 2, 1, 3).reshape(n_chunks, P, TILES * SPH),
    }
    attr = edges(a["edge_attr_16"])
    arrays["attr0"] = attr.reshape(n_chunks, 2, 2, P, -1).transpose(0, 2, 4, 1, 3).reshape(n_chunks, -1, 2 * P)
    arrays["attr1"] = edges(a["edge_attr_10"]).reshape(n_chunks, CHUNK, -1).transpose(0, 2, 1)
    l2s, l2v = a["L0_gnn_Wl2_s"], a["L0_gnn_Wl2_v"]
    weights = [
        {"fc1": a["L0_gnn_Wfc1"], "fc2": a["L0_gnn_Wfc2"], "t0": a["L0_gnn_Wl1_0"], "t1": a["L0_gnn_Wl1_1"],
         "s0": a["L0_gnn_Wsc0"], "s1": a["L0_gnn_Wsc1"], "a": l2s[:MUL0], "dd": l2s[MUL0:],
         "b": l2v[:MUL0], "c": l2v[MUL0:], "alpha": a["L0_gnn_Wa"]},
        {"fc1": a["L1_gnn_W_fc1"], "fc2": a["L1_gnn_W_fc2"], "t0": a["L1_gnn_W_l1_0"], "t1": a["L1_gnn_W_l1_1"],
         "s0": a["L1_gnn_W_si0"], "s1": a["L1_gnn_W_si1"], "a": a["L1_gnn_W_l2_00"], "dd": a["L1_gnn_W_l2_10"],
         "b": a["L1_gnn_W_l2_01"], "c": a["L1_gnn_W_l2_11"]},
    ]
    for l in range(2):
        arrays.update({f"L{l}_{k}": v for k, v in weights[l].items()})
    arrays = {f"in_{k}": np.ascontiguousarray(v) for k, v in arrays.items()}

    nc = bacc.Bacc("TRN2", target_bir_lowering=False, num_devices=1)
    d = {k[3:]: nc.dram_tensor(k, v.shape, mb.dt.from_np(v.dtype), kind="ExternalInput").ap()
         for k, v in arrays.items()}
    for name in ("table0", "resid0", "table1", "resid1"):
        d[name] = nc.dram_tensor(name, (n_rows, FEAT), mb.dt.float32, kind="Internal").ap()
    d["out"] = nc.dram_tensor("out_0", (n_rows, FEAT), mb.dt.float32, kind="ExternalOutput").ap()
    build(nc, d, n_nodes, n_chunks, n_ntiles)
    got = run_bass_kernel_spmd(nc, [arrays], core_ids=[0]).results[0]["out_0"][:n_nodes]
    vectors = got[:, MUL0:].reshape(-1, VEC, MUL1).transpose(0, 2, 1).reshape(-1, VEC * MUL1)
    return np.concatenate([got[:, :MUL0], vectors], axis=1)
```
